# Optimizing a Trainium2 kernel written in Bass

```python
import numpy as np
import jax
import jax.numpy as jnp

def _softmax(x, axis=-1):
    return jax.nn.softmax(x, axis=axis)

def _gelu(x):
    return jax.nn.gelu(x, approximate=True)

def _silu(x):
    return jax.nn.silu(x)

def _sigmoid(x):
    return jax.nn.sigmoid(x)

def _layernorm(x, axis=-1, eps=1e-05):
    m = jnp.mean(x, axis=axis, keepdims=True)
    v = jnp.var(x, axis=axis, keepdims=True)
    return (x - m) / jnp.sqrt(v + eps)

def _scatter_add(tgt, idx, src, axis=0):
    return tgt.at[idx].add(src)

def _segment_sum(src, seg, n):
    return jax.ops.segment_sum(src, seg, n)
kernel_name = 'mk_adj_preln_d2_adj_r2_011882'

def setup_inputs(seed: int=0):
    np.random.seed(seed)
    _w = jnp.asarray

    def _rec_inputs():
        import jax
        import jax.numpy as jnp
        _gk = jax.random.key(seed)
        x = -0.0005207 + 1.001 * jax.random.normal(jax.random.fold_in(_gk, 1), (8, 1024, 128), jnp.float32)
        _a = jax.random.bernoulli(jax.random.fold_in(_gk, 2), 0.0078125, (8, 1024, 1024))
        _a = jnp.logical_or(_a, jnp.swapaxes(_a, -1, -2))
        _a = jnp.logical_or(_a, jnp.eye(1024, dtype=bool))
        _af = _a.astype(jnp.float32)
        _af = _af * jax.random.uniform(jax.random.fold_in(_gk, 3), (8, 1024, 1024), jnp.float32, 0.05, 1)
        adj = _af
        return (x, adj)
    x, adj = _rec_inputs()

    def _L0_gnn_setup():
        import jax, jax.numpy as jnp
        import numpy as np
        key = jax.random.key(seed)
        k1, k2, k3, k4 = jax.random.split(key, 4)
        B, N, D = (8, 1024, 128)
        embeddings = jax.random.normal(k1, (B, N, D), dtype=jnp.float32)
        adjacency_matrix = jax.random.uniform(k2, (B, N, N), dtype=jnp.float32)
        cost_matrix = jax.random.uniform(k3, (B, N, N), dtype=jnp.float32)
        W = jax.random.normal(k4, (D, 2 * D), dtype=jnp.float32) * (1.0 / np.sqrt(2 * D))
        b = jnp.zeros((D,), dtype=jnp.float32)
        return {'embeddings': embeddings, 'adjacency_matrix': adjacency_matrix, 'cost_matrix': cost_matrix, 'W': W, 'b': b}
    _L0_gnn_all = _L0_gnn_setup()
    _L0_gnn_in = {k: v for k, v in _L0_gnn_all.items() if k in ('W', 'b')}
    del _L0_gnn_all

    def _L1_gnn_setup():
        import jax, jax.numpy as jnp
        import numpy as np
        EPS = 1e-12

        def _adapt_conv(h, edge_weight, W, b, is_last):
            h = h @ W + b
            norm = jnp.linalg.norm(h, axis=-1, keepdims=True)
            nh = h / jnp.maximum(norm, EPS)
            cos = jnp.einsum('bij,bkj->bik', nh, nh)
            ew = edge_weight * cos
            h = jnp.einsum('bpq,bqc->bpc', ew, h)
            if not is_last:
                h = jax.nn.relu(h)
            return h
        key = jax.random.key(seed)
        ks = jax.random.split(key, 8)
        B, N, D, H = (8, 1024, 128, 128)
        s = 1.0 / np.sqrt(D)
        return {'x': jax.random.normal(ks[0], (B, N, D), dtype=jnp.float32), 'edge_weight': jax.random.uniform(ks[1], (B, N, N), dtype=jnp.float32), 'W0': jax.random.normal(ks[2], (D, H), dtype=jnp.float32) * s, 'b0': jnp.zeros((H,), dtype=jnp.float32), 'W1': jax.random.normal(ks[3], (H, H), dtype=jnp.float32) * s, 'b1': jnp.zeros((H,), dtype=jnp.float32), 'W2': jax.random.normal(ks[4], (H, H), dtype=jnp.float32) * s, 'b2': jnp.zeros((H,), dtype=jnp.float32)}
    _L1_gnn_all = _L1_gnn_setup()
    _L1_gnn_in = {k: v for k, v in _L1_gnn_all.items() if k in ('W0', 'b0', 'W1', 'b1', 'W2', 'b2')}
    del _L1_gnn_all
    return {'x': x, 'adj': adj, 'L0_gnn_W': _L0_gnn_in['W'], 'L0_gnn_b': _L0_gnn_in['b'], 'L1_gnn_W0': _L1_gnn_in['W0'], 'L1_gnn_b0': _L1_gnn_in['b0'], 'L1_gnn_W1': _L1_gnn_in['W1'], 'L1_gnn_b1': _L1_gnn_in['b1'], 'L1_gnn_W2': _L1_gnn_in['W2'], 'L1_gnn_b2': _L1_gnn_in['b2']}

def reference(x, adj, L0_gnn_W, L0_gnn_b, L1_gnn_W0, L1_gnn_b0, L1_gnn_W1, L1_gnn_b1, L1_gnn_W2, L1_gnn_b2):
    import jax
    import jax.numpy as jnp

    def _L0_gnn_ref(embeddings, adjacency_matrix, cost_matrix, W, b):
        import jax, jax.numpy as jnp
        import numpy as np
        degree = adjacency_matrix.sum(axis=-1)[:, :, None]
        sum_neighbors = jnp.einsum('bid,bij->bjd', embeddings, cost_matrix) / degree
        concatenated = jnp.concatenate([embeddings, sum_neighbors], axis=-1)
        out = jnp.einsum('bnk,dk->bnd', concatenated, W) + b
        return jax.nn.relu(out)

    def _L1_gnn_ref(x, edge_weight, W0, b0, W1, b1, W2, b2):
        import jax, jax.numpy as jnp
        import numpy as np
        EPS = 1e-12

        def _adapt_conv(h, edge_weight, W, b, is_last):
            h = h @ W + b
            norm = jnp.linalg.norm(h, axis=-1, keepdims=True)
            nh = h / jnp.maximum(norm, EPS)
            cos = jnp.einsum('bij,bkj->bik', nh, nh)
            ew = edge_weight * cos
            h = jnp.einsum('bpq,bqc->bpc', ew, h)
            if not is_last:
                h = jax.nn.relu(h)
            return h
        params = [(W0, b0), (W1, b1), (W2, b2)]
        h = x
        n_layers = len(params)
        for i, (W, b) in enumerate(params):
            h = _adapt_conv(h, edge_weight, W, b, is_last=i == n_layers - 1)
        return h
    h = jnp.maximum(_layernorm(x, axis=-1), 0.0)
    x = x + _L0_gnn_ref(h, adj, adj, L0_gnn_W, L0_gnn_b)
    h = jnp.maximum(_layernorm(x, axis=-1), 0.0)
    x = x + _L1_gnn_ref(h, adj, L1_gnn_W0, L1_gnn_b0, L1_gnn_W1, L1_gnn_b1, L1_gnn_W2, L1_gnn_b2)
    return x

_drawn_inputs = setup_inputs


def setup_inputs(seed=0):
    import zlib

    import numpy as np

    out = dict(_drawn_inputs(seed))
    spreads = {'L0_gnn_b': (0.0, 0.1),
     'L1_gnn_b0': (0.0, 0.1),
     'L1_gnn_b1': (0.0, 0.1),
     'L1_gnn_b2': (0.0, 0.322)}
    factors = {}
    for name, (base, spread) in spreads.items():
        noise = np.random.default_rng([zlib.crc32(name.encode()), seed]).standard_normal(out[name].shape)
        drawn = base * np.exp(spread * noise) if base else spread * noise
        out[name] = jnp.asarray(drawn.astype(out[name].dtype))
    for name, factor in factors.items():
        out[name] = (out[name] * factor).astype(out[name].dtype)
    return out
```

```python
from contextlib import ExitStack

import concourse.bass as bass
from concourse import mybir

ALU = mybir.AluOpType
ACT = mybir.ActivationFunctionType
F32 = mybir.dt.float32
F32R = mybir.dt.float32r
AX = mybir.AxisListType.X

P = 128
SLOTS = 32
HI_AHEAD, LO_AHEAD, COS_AHEAD = 2, 1, 3
RING = 4
PHASE_AT = {2: 0, 1: 8, 0: 16, 3: 24}
LAG = {2: 2, 1: 1, 0: 0, 3: 2}
LN_EPS = 1e-5
NORM_EPS = 1e-12


def build(nc, x, adj, adj_t, consts, out):
    B, N, D = x.shape
    NT = N // P
    HALF = N // 2
    assert D == P and NT == 8 and SLOTS == 4 * NT and B % 2 == 0 and B > 3
    PAIRS = NT // 2
    LAST = B + 1

    class Cycle:
        def __init__(self, k, i=None):
            self.k, self.i = k, i

        def graph(self, lag):
            return self.k - lag + (0 if self.i is None else 2 * self.i)

        def has(self, lag):
            return 0 <= self.k - lag < B

        def next(self):
            return Cycle(self.k + 1, self.i)

    def phase_of(slot):
        return next(f for f in PHASE_AT if PHASE_AT[f] <= slot < PHASE_AT[f] + NT)

    def active(k):
        return [s for s in range(SLOTS) if 0 <= k - LAG[phase_of(s)] < B]

    def before(c, per_cycle):
        n = sum(per_cycle(k) for k in range(c.k))
        return n if c.i is None else n + 2 * per_cycle(3) * c.i

    def item(c, s):
        return before(c, lambda k: len(active(k))) + active(c.k).index(s)

    def is_cos(s):
        return phase_of(s) != 0

    def cos_item(c, s):
        return (before(c, lambda k: sum(map(is_cos, active(k))))
                + sum(is_cos(t) for t in active(c.k) if t < s))

    def lo_on_dve(s):
        return not is_cos(s) and s % 2 == 1

    def lows(c, s, dve):
        return (before(c, lambda k: sum(lo_on_dve(t) == dve for t in active(k)))
                + sum(lo_on_dve(t) == dve for t in active(c.k) if t < s))

    def phases_before(c, f):
        return (before(c, lambda k: len(active(k)) // NT)
                + sum(c.has(LAG[g]) for g in PHASE_AT if PHASE_AT[g] < PHASE_AT[f]))

    JOBS = [("E", 0), ("D", 2), ("A", 1), ("Bn", 0), ("B", 0)]
    SPLITS = [("B", 1), ("E", 0), ("D", 2), ("A", 1)]
    NHTS = [("B", 1), ("D", 2), ("A", 1)]
    STAGES = [("B_nhT", 1), ("E_hT", 0), ("E_e", 0), ("D_H", 2), ("D_nhT", 2), ("A_H", 1),
              ("A_nhT", 1), ("B_z", 0), ("B_hT", 0), ("B_H", 0), ("C_out", 2)]

    def nth(events, c, name):
        n = before(c, lambda k: sum(0 <= k - lag < B for _, lag in events))
        for e, lag in events:
            if e == name:
                return n
            n = n + int(c.has(lag))
        return n

    ctx = ExitStack()
    with ctx:
        def sb(name, shape, dt=F32):
            return ctx.enter_context(nc.sbuf_tensor(name, shape, dt))

        def sem(name):
            return ctx.enter_context(nc.semaphore(name))

        adj_sb = sb("adj_sb", [P, NT, N])
        adjt_sb = [sb(f"adjt_sb{p}", [P, NT, N]) for p in range(2)]
        ew = sb("ew", [P, 2, N])
        mov_hi = sb("mov_hi", [P, RING, N], F32R)
        mov_lo = sb("mov_lo", [P, RING, N], F32R)
        sta_hi = [sb(f"sta_hi{i}", [P, N], F32R) for i in range(2)]
        sta_lo = [sb(f"sta_lo{i}", [P, N], F32R) for i in range(2)]
        nht_hi = [sb(f"nht_hi{i}", [P, N], F32R) for i in range(2)]
        nht_lo = [sb(f"nht_lo{i}", [P, N], F32R) for i in range(2)]
        x_sb = sb("x_sb", [P, NT, D])
        x1_sb = sb("x1_sb", [P, NT, D])
        park = [sb(f"park{p}", [P, NT, D]) for p in range(2)]
        yt = sb("yt", [P, N])
        val = sb("val", [P, NT, D])
        scr = sb("scr", [P, NT, D])
        e_sb = sb("e_sb", [P, NT, D])
        cst = sb("cst", [P, consts.shape[1]])
        deg = sb("deg", [P, NT])
        rdeg = sb("rdeg", [P, NT])
        rsum = sb("rsum", [P, NT])
        ssum = sb("ssum", [P, NT])
        var = sb("var", [P, NT])
        rstd = sb("rstd", [P, NT])
        expo = sb("expo", [P, NT])

        w = [cst[:, i * D:(i + 1) * D] for i in range(3)]
        wa_t, wb_t = cst[:, 3 * D:4 * D], cst[:, 4 * D:5 * D]
        bias = [cst[:, (5 + i) * D:(6 + i) * D].unsqueeze(1).to_broadcast([P, NT, D]) for i in range(3)]
        bias_l0 = cst[:, 8 * D:9 * D].unsqueeze(1).to_broadcast([P, NT, D])
        ident = cst[:, 9 * D:10 * D]

        gram = ctx.enter_context(nc.psum_tensor("gram", [P, 2, N], F32))
        ysum = ctx.enter_context(nc.psum_tensor("ysum", [P, N], F32))
        stage = ctx.enter_context(nc.psum_tensor("stage", [P, NT, D], F32))

        const_in = sem("const_in")
        x_in = sem("x_in")
        adj_in = [sem(f"adj_in{g}") for g in range(PAIRS)]
        adjt_in = [[sem(f"adjt_in{p}_{g}") for g in range(PAIRS)] for p in range(2)]
        parked = sem("parked")
        out_done = sem("out_done")
        expo_set = sem("expo_set")
        cos_done = sem("cos_done")
        ew_done = sem("ew_done")
        hi_done = sem("hi_done")
        lo_dve = sem("lo_dve")
        lo_pool = sem("lo_pool")
        item_done = sem("item_done")
        y_read = sem("y_read")
        stage_full = sem("stage_full")
        stage_read = sem("stage_read")
        centred = sem("centred")
        sq_done = sem("sq_done")
        ss_done = sem("ss_done")
        var_done = sem("var_done")
        rstd_done = sem("rstd_done")
        nrm_done = sem("nrm_done")
        rsum_done = sem("rsum_done")
        sta_hi_done = sem("sta_hi_done")
        sta_lo_done = sem("sta_lo_done")
        nht_hi_done = sem("nht_hi_done")
        h_done = sem("h_done")
        rdeg_done = sem("rdeg_done")
        ze_done = sem("ze_done")
        x1_done = sem("x1_done")

        def tiles(ap):
            return ap.rearrange("p (t d) -> p t d", t=NT)

        def rows(dram, b):
            return dram[b].rearrange("(t p) d -> p t d", p=P)

        def run(eng, cycle):
            for k in (0, 1):
                cycle(Cycle(k))
            with eng.Fori(0, (B - 2) // 2) as i:
                for k in (2, 3):
                    cycle(Cycle(k, i))
            for k in range(B, LAST + 1):
                cycle(Cycle(k))

        def at(c, s):
            c, s = (c, s) if s < SLOTS else (c.next(), s - SLOTS)
            return (c, s) if s in active(c.k) else None

        block = ctx.enter_context(nc.Block())

        @block.sync
        def _(sp):
            sp.dma_start(cst[:, :], consts[:, :]).then_inc(const_in, 16)

            def cycle(c):
                if c.has(0):
                    b = c.graph(0)
                    if c.k > 0:
                        sp.wait_ge(x1_done, b)
                    sp.dma_start(x_sb[:, :, :], rows(x, b)).then_inc(x_in, 16)
                    if c.k > 0:
                        sp.wait_ge(item_done, item_end(c))
                    for g in range(PAIRS):
                        sp.dma_start(adj_sb[:, 2 * g:2 * g + 2, :],
                                     rows(adj, b)[:, 2 * g:2 * g + 2, :]).then_inc(adj_in[g], 16)
                    for g in range(PAIRS):
                        if c.has(2):
                            sp.wait_ge(ew_done, cos_item(c, PHASE_AT[3] + 2 * g + 1) + 1)
                        sp.dma_start(adjt_sb[c.k % 2][:, 2 * g:2 * g + 2, :],
                                     rows(adj_t, b)[:, 2 * g:2 * g + 2, :]).then_inc(adjt_in[c.k % 2][g], 16)
                if c.has(2):
                    sp.wait_ge(stage_read, nth(STAGES, c, "C_out") + 1)
                    sp.dma_start(rows(out, c.graph(2)), park[c.k % 2][:, :, :]).then_inc(out_done, 16)
                if c.has(0):
                    if c.has(2):
                        sp.wait_ge(out_done, 16 * (c.graph(2) + 1))
                    else:
                        sp.wait_ge(x1_done, c.graph(0) + 1)
                    sp.dma_start(park[c.k % 2][:, :, :], x1_sb[:, :, :]).then_inc(parked, 16)

            def item_end(c):
                return before(c, lambda k: len(active(k)))

            run(sp, cycle)
            sp.wait_ge(out_done, 16 * B)

        @block.tensor
        def _(pe):
            def cosines(now, c, s):
                q, f = s % NT, phase_of(s)
                hi, lo = nht_hi[f % 2], nht_lo[f % 2]
                n = cos_item(c, s)
                if q == 0:
                    made = {2: "A_nhT", 1: "B_nhT", 3: "D_nhT"}[f]
                    pe.wait_ge(stage_read, nth(STAGES, now if f == 2 else c, made) + 1)
                if not (c.i is None and n < 2):
                    pe.wait_ge(ew_done, n - 1)
                cols = slice(q * P, (q + 1) * P)
                for sta, mov, first, last in ((lo, hi, True, False), (hi, lo, False, False), (hi, hi, False, True)):
                    for h in range(2):
                        part = slice(h * HALF, (h + 1) * HALF)
                        mm = nc.tensor.matmul(gram[:, q % 2, part], sta[:, cols], mov[:, part],
                                              start=first, stop=last)
                mm.then_inc(cos_done, 1)

            def sum_item(c, s):
                q, f = s % NT, phase_of(s)
                hi, lo = sta_hi[f % 2], sta_lo[f % 2]
                if q == 0:
                    n = {2: nth(SPLITS, c, "B"), 1: nth(SPLITS, c, "B") + 1,
                         0: nth(SPLITS, c, "E") + 1, 3: nth(SPLITS, c, "D") + 1}[f]
                    pe.wait_ge(sta_hi_done, n)
                    pe.wait_ge(sta_lo_done, n)
                    if not (c.i is None and phases_before(c, f) == 0):
                        pe.wait_ge(y_read, phases_before(c, f))
                cols = slice(q * P, (q + 1) * P)
                pe.wait_ge(hi_done, item(c, s) + 1)
                for sta, mov in ((hi, mov_hi), (lo, mov_hi), (hi, mov_lo)):
                    if mov is mov_lo:
                        dve = lo_on_dve(s)
                        pe.wait_ge(lo_dve if dve else lo_pool, lows(c, s, dve) + 1)
                    for h in range(2):
                        part = slice(h * HALF, (h + 1) * HALF)
                        mm = nc.tensor.matmul(ysum[:, part], sta[:, cols], mov[:, q % RING, part],
                                              start=(q == 0 and sta is hi and mov is mov_hi),
                                              stop=(q == NT - 1 and mov is mov_lo))
                mm.then_inc(item_done, 1)

            def stage_free(c, name):
                n = nth(STAGES, c, name)
                if not (c.i is None and n == 0):
                    pe.wait_ge(stage_read, n)

            def rows_times(ft, weights):
                for t in range(NT):
                    mm = nc.tensor.matmul(stage[:, t, :], ft[:, t * P:(t + 1) * P], weights,
                                          start=True, stop=True)
                mm.then_inc(stage_full, 1)

            def transposes(src):
                for t in range(NT):
                    mm = nc.tensor.transpose(stage[:, t, :], src(t), ident)
                mm.then_inc(stage_full, 1)

            def cycle(c):
                job_nrm = before(c, lambda k: sum(0 <= k - lag < B for _, lag in JOBS))
                for s in range(SLOTS):
                    if at(c, s):
                        sum_item(c, s)
                    if (ahead := at(c, s + COS_AHEAD)) and is_cos(ahead[1]):
                        cosines(c, *ahead)
                    if s == 1 and c.has(1):
                        stage_free(c, "B_nhT")
                        pe.wait_ge(nrm_done, job_nrm)
                        transposes(lambda t: scr[:, t, :])
                    if s == 8 and c.has(0):
                        stage_free(c, "E_hT")
                        pe.wait_ge(h_done, c.graph(0) + 1)
                        transposes(lambda t: val[:, t, :])
                    if s == 9 and c.has(0):
                        stage_free(c, "E_e")
                        pe.wait_ge(stage_read, nth(STAGES, c, "E_hT") + 1)
                        rows_times(e_sb[:, :, :].rearrange("p t d -> p (t d)"), wa_t)
                    if s == 10 and c.has(2):
                        stage_free(c, "D_H")
                        pe.wait_ge(y_read, phases_before(c, 1))
                        rows_times(yt[:, :], w[2])
                    if s == 13 and c.has(2):
                        stage_free(c, "D_nhT")
                        pe.wait_ge(nrm_done, nth(JOBS, c, "D") + 1)
                        transposes(lambda t: scr[:, t, :])
                    if s == 17 and c.has(1):
                        stage_free(c, "A_H")
                        pe.wait_ge(y_read, phases_before(c, 0))
                        rows_times(yt[:, :], w[1])
                    if s == 20 and c.has(1):
                        stage_free(c, "A_nhT")
                        pe.wait_ge(nrm_done, nth(JOBS, c, "A") + 1)
                        transposes(lambda t: scr[:, t, :])
                    if s == 24 and c.has(0):
                        stage_free(c, "B_z")
                        pe.wait_ge(y_read, phases_before(c, 3))
                        rows_times(yt[:, :], wb_t)
                    if s == 28 and c.has(0):
                        stage_free(c, "B_hT")
                        pe.wait_ge(nrm_done, nth(JOBS, c, "Bn") + 1)
                        transposes(lambda t: scr[:, t, :])
                    if s == 29 and c.has(0):
                        stage_free(c, "B_H")
                        pe.wait_ge(stage_read, nth(STAGES, c, "B_hT") + 1)
                        rows_times(yt[:, :], w[0])
                    if s == 31 and c.has(2):
                        stage_free(c, "C_out")
                        pe.wait_ge(y_read, phases_before(c, 3) + 1)
                        transposes(lambda t: yt[:, t * P:(t + 1) * P])

            pe.wait_ge(const_in, 16)
            run(pe, cycle)

        @block.vector
        def _(dve):
            def times_adj(c, s):
                q, f = s % NT, phase_of(s)
                parity = (c.k - LAG[f]) % 2
                if f == 1 and q % 2 == 0:
                    dve.wait_ge(adjt_in[parity][q // 2],
                                16 * ((c.k - 1) // 2 + 1 + (0 if c.i is None else c.i)))
                dve.wait_ge(cos_done, cos_item(c, s) + 1)
                if not (c.i is None and cos_item(c, s) < 2):
                    order = active(c.k)
                    dve.wait_ge(hi_done, item(c, s) - 1)
                    pos = order.index(s)
                    if pos >= 1:
                        dve.wait_ge(lo_pool, lows(c, order[pos - 1], False))
                        if not is_cos(order[pos - 1]):
                            dve.wait_ge(lo_dve, lows(c, order[pos - 1], True))
                    else:
                        dve.wait_ge(lo_pool, lows(c, s, False) - 1)
                nc.vector.tensor_tensor(ew[:, q % 2, :], adjt_sb[parity][:, q, :], gram[:, q % 2, :],
                                        ALU.mult).then_inc(ew_done, 1)

            def low_part(c, s):
                q = s % NT
                n = item(c, s)
                dve.wait_ge(hi_done, n + 1)
                if not (c.i is None and n < RING):
                    dve.wait_ge(item_done, n - RING + 1)
                nc.vector.tensor_tensor(mov_lo[:, q % RING, :], adj_sb[:, q, :],
                                        mov_hi[:, q % RING, :].bitcast(F32), ALU.subtract).then_inc(lo_dve, 1)

            def bc(ap):
                return ap.unsqueeze(2).to_broadcast([P, NT, D])

            def val_free(c, name):
                n = nth(SPLITS, c, {"E": "E", "D": "D", "A": "A"}.get(name))
                if not (c.i is None and n == 0):
                    dve.wait_ge(sta_hi_done, n)
                    dve.wait_ge(sta_lo_done, n)

            def centre(c, job, src, which):
                nc.vector.tensor_reduce(rsum[:, :], src[:, :, :], AX, ALU.add).then_inc(rsum_done, 1)
                dve.wait_ge(rsum_done, which)
                val_free(c, job)
                nc.vector.scalar_tensor_tensor(out=val[:, :, :], in0=bc(rsum[:, :]), scalar=-1.0 / D,
                                               in1=src[:, :, :], op0=ALU.mult, op1=ALU.add).then_inc(centred, 1)

            def variance(n, layernorm):
                dve.wait_ge(sq_done, n)
                nc.vector.tensor_reduce(ssum[:, :], scr[:, :, :], AX, ALU.add).then_inc(ss_done, 1)
                dve.wait_ge(ss_done, n)
                if layernorm:
                    nc.vector.tensor_scalar(var[:, :], ssum[:, :], 1.0 / D, LN_EPS, ALU.mult,
                                            ALU.add).then_inc(var_done, 1)
                else:
                    nc.vector.tensor_scalar(var[:, :], ssum[:, :], NORM_EPS * NORM_EPS, None,
                                            ALU.max).then_inc(var_done, 1)

            def normalise(n):
                dve.wait_ge(rstd_done, n)
                nc.vector.tensor_tensor(scr[:, :, :], val[:, :, :], bc(rstd[:, :]),
                                        ALU.mult).then_inc(nrm_done, 1)

            def make_h(c, stage_name, job, b):
                dve.wait_ge(stage_full, nth(STAGES, c, stage_name) + 1)
                val_free(c, job)
                nc.vector.tensor_tensor(val[:, :, :], stage[:, :, :], b, ALU.add).then_inc(stage_read, 1)

            def nht_low(c, stage_name, name, i):
                dve.wait_ge(nht_hi_done, nth(NHTS, c, name) + 1)
                nc.vector.tensor_tensor(tiles(nht_lo[i][:, :]), stage[:, :, :],
                                        tiles(nht_hi[i][:, :]).bitcast(F32), ALU.subtract)\
                    .then_inc(stage_read, 1)

            def cycle(c):
                last_job = before(c, lambda k: sum(0 <= k - lag < B for _, lag in JOBS))
                for s in range(SLOTS):
                    if (ahead := at(c, s + HI_AHEAD)) and is_cos(ahead[1]):
                        times_adj(*ahead)
                    if (ahead := at(c, s + LO_AHEAD)) and lo_on_dve(ahead[1]):
                        low_part(*ahead)
                    if s == 0 and c.has(1):
                        variance(last_job, False)
                    if s == 1 and c.has(1):
                        normalise(last_job)
                    if s == 2 and c.has(1):
                        nht_low(c, "B_nhT", "B", 1)
                    if s == 4 and c.has(0):
                        dve.wait_ge(x_in, 16 * (c.graph(0) + 1))
                        centre(c, "E", x_sb, nth_ln(c, 0))
                    if s == 6 and c.has(0):
                        variance(nth(JOBS, c, "E") + 1, True)
                    if s == 7 and c.has(0):
                        normalise(nth(JOBS, c, "E") + 1)
                    if s == 9 and c.has(0):
                        dve.wait_ge(stage_full, nth(STAGES, c, "E_e") + 1)
                        nc.vector.tensor_tensor(e_sb[:, :, :], stage[:, :, :], bias_l0,
                                                ALU.add).then_inc(stage_read, 1)
                    if s == 10 and c.has(2):
                        make_h(c, "D_H", "D", bias[2])
                    if s == 12 and c.has(2):
                        variance(nth(JOBS, c, "D") + 1, False)
                    if s == 13 and c.has(2):
                        normalise(nth(JOBS, c, "D") + 1)
                    if s == 14 and c.has(2):
                        nht_low(c, "D_nhT", "D", 1)
                    if s == 17 and c.has(1):
                        make_h(c, "A_H", "A", bias[1])
                    if s == 19 and c.has(1):
                        variance(nth(JOBS, c, "A") + 1, False)
                    if s == 20 and c.has(1):
                        normalise(nth(JOBS, c, "A") + 1)
                    if s == 21 and c.has(1):
                        nht_low(c, "A_nhT", "A", 0)
                    if s == 24 and c.has(0):
                        b = c.graph(0)
                        dve.wait_ge(y_read, phases_before(c, 3))
                        nc.vector.reciprocal(rdeg[:, :], deg[:, :]).then_inc(rdeg_done, 1)
                        dve.wait_ge(rdeg_done, b + 1)
                        dve.wait_ge(stage_full, nth(STAGES, c, "B_z") + 1)
                        nc.vector.tensor_tensor(scr[:, :, :], stage[:, :, :], bc(rdeg[:, :]), ALU.mult)\
                            .then_inc(stage_read, 1)
                        dve.wait_ge(stage_read, nth(STAGES, c, "B_z") + 1)
                        nc.vector.tensor_tensor(scr[:, :, :], scr[:, :, :], e_sb[:, :, :],
                                                ALU.add).then_inc(ze_done, 1)
                        dve.wait_ge(ze_done, b + 1)
                        if c.k > 0:
                            dve.wait_ge(parked, 16 * b)
                        nc.vector.scalar_tensor_tensor(out=x1_sb[:, :, :], in0=scr[:, :, :], scalar=0.0,
                                                       in1=x_sb[:, :, :], op0=ALU.max,
                                                       op1=ALU.add).then_inc(x1_done, 1)
                    if s == 25 and c.has(0):
                        dve.wait_ge(x1_done, c.graph(0) + 1)
                        centre(c, "Bn", x1_sb, nth_ln(c, 1))
                    if s == 27 and c.has(0):
                        variance(nth(JOBS, c, "Bn") + 1, True)
                    if s == 28 and c.has(0):
                        normalise(nth(JOBS, c, "Bn") + 1)
                    if s == 29 and c.has(0):
                        make_h(c, "B_H", "B", bias[0])
                    if s == 31 and c.has(2):
                        b = c.graph(2)
                        dve.wait_ge(parked, 16 * (b + 1))
                        dve.wait_ge(stage_full, nth(STAGES, c, "C_out") + 1)
                        nc.vector.tensor_tensor(park[c.k % 2][:, :, :], stage[:, :, :],
                                                park[c.k % 2][:, :, :], ALU.add)\
                            .then_inc(stage_read, 1)

            def nth_ln(c, second):
                return 2 * c.graph(0) + 1 + second

            dve.wait_ge(const_in, 16)
            run(dve, cycle)

        @block.scalar
        def _(act):
            def high_part(c, s):
                q, n = s % NT, item(c, s)
                if is_cos(s):
                    act.wait_ge(ew_done, cos_item(c, s) + 1)
                    src = ew[:, q % 2, :]
                else:
                    if q % 2 == 0:
                        act.wait_ge(adj_in[q // 2], 16 * (c.graph(0) + 1))
                    src = adj_sb[:, q, :]
                if not (c.i is None and n < RING):
                    act.wait_ge(item_done, n - RING + 1)
                if is_cos(s):
                    nc.scalar.activation(mov_hi[:, q % RING, :], src, ACT.Copy).then_inc(hi_done, 1)
                else:
                    nc.scalar.activation(mov_hi[:, q % RING, :], src, ACT.Identity,
                                         accum_out=deg[:, q:q + 1]).then_inc(hi_done, 1)

            def read_sum(c, f):
                s = PHASE_AT[f] + NT - 1
                act.wait_ge(item_done, item(c, s) + 1)
                prior = {2: "E_hT", 1: "A_H", 0: "B_z", 3: "C_out"}[f]
                n = nth(STAGES, c, prior)
                if not (c.i is None and n == 0):
                    act.wait_ge(stage_full, n)
                nc.scalar.activation(yt[:, :], ysum[:, :], ACT.Relu if f in (1, 2) else ACT.Copy)\
                    .then_inc(y_read, 1)

            def squares(c, job):
                if job in ("E", "Bn"):
                    act.wait_ge(centred, 2 * c.graph(0) + 1 + (job == "Bn"))
                else:
                    act.wait_ge(stage_read, nth(STAGES, c, job + "_H") + 1)
                prior = {"E": "E_hT", "D": "D_nhT", "A": "A_nhT", "Bn": "B_hT", "B": "C_out"}[job]
                n = nth(STAGES, c, prior)
                if not (c.i is None and n == 0):
                    act.wait_ge(stage_full, n)
                nc.scalar.activation(scr[:, :, :], val[:, :, :], ACT.Square).then_inc(sq_done, 1)

            def sta_high(i, n, done):
                if n is not None:
                    act.wait_ge(item_done, n)
                nc.scalar.activation(tiles(sta_hi[i][:, :]), val[:, :, :], ACT.Copy).then_inc(sta_hi_done, 1)

            def nht_high(c, stage_name, i):
                act.wait_ge(stage_full, nth(STAGES, c, stage_name) + 1)
                nc.scalar.activation(tiles(nht_hi[i][:, :]), stage[:, :, :], ACT.Copy).then_inc(nht_hi_done, 1)

            def cycle(c):
                for s in range(SLOTS):
                    if ahead := at(c, s + HI_AHEAD):
                        high_part(*ahead)
                    if s == 0 and c.has(1):
                        sta_high(1, items_before(c), None)
                    if s == 2 and c.has(1):
                        nht_high(c, "B_nhT", 1)
                    if s == 5 and c.has(0):
                        squares(c, "E")
                    if s == 7 and c.has(2):
                        read_sum(c, 2)
                    if s == 8 and c.has(0):
                        act.wait_ge(nrm_done, nth(JOBS, c, "E") + 1)
                        nc.scalar.activation(val[:, :, :], scr[:, :, :], ACT.Relu).then_inc(h_done, 1)
                        act.wait_ge(h_done, c.graph(0) + 1)
                        sta_high(0, item(c, 7) + 1 if c.has(2) else items_before(c) if c.k > 0 else None, None)
                        act.wait_ge(stage_full, nth(STAGES, c, "E_hT") + 1)
                        nc.scalar.activation(e_sb[:, :, :], stage[:, :, :], ACT.Copy)\
                            .then_inc(stage_read, 1)
                    if s == 11 and c.has(2):
                        squares(c, "D")
                    if s == 14 and c.has(2):
                        nht_high(c, "D_nhT", 1)
                    if s == 15 and c.has(1):
                        read_sum(c, 1)
                    if s == 16 and c.has(2):
                        sta_high(1, item(c, 15) + 1 if c.has(1) else item(c, 7) + 1, None)
                    if s == 18 and c.has(1):
                        squares(c, "A")
                    if s == 21 and c.has(1):
                        nht_high(c, "A_nhT", 0)
                    if s == 23 and c.has(0):
                        read_sum(c, 0)
                    if s == 24 and c.has(1):
                        sta_high(0, item(c, 23) + 1 if c.has(0) else item(c, 15) + 1, None)
                    if s == 26 and c.has(0):
                        squares(c, "Bn")
                    if s == 28 and c.has(0):
                        act.wait_ge(stage_full, nth(STAGES, c, "B_hT") + 1)
                        nc.scalar.activation(yt[:, :], stage[:, :, :].rearrange("p t d -> p (t d)"), ACT.Relu)\
                            .then_inc(stage_read, 1)
                    if s == 30 and c.has(0):
                        squares(c, "B")
                    if s == 31 and c.has(2):
                        read_sum(c, 3)

            def items_before(c):
                return before(c, lambda k: len(active(k)))

            run(act, cycle)

        @block.gpsimd
        def _(pool):
            def low_part(c, s):
                q, n = s % NT, item(c, s)
                pool.wait_ge(hi_done, n + 1)
                if not (c.i is None and n < RING):
                    pool.wait_ge(item_done, n - RING + 1)
                src = ew[:, q % 2, :] if is_cos(s) else adj_sb[:, q, :]
                nc.gpsimd.tensor_tensor(mov_lo[:, q % RING, :], src, mov_hi[:, q % RING, :].bitcast(F32),
                                        ALU.subtract).then_inc(lo_pool, 1)

            def power(n):
                pool.wait_ge(var_done, n)
                nc.gpsimd.tensor_tensor(rstd[:, :], var[:, :], expo[:, :], ALU.pow).then_inc(rstd_done, 1)

            def sta_low(c, i, name):
                pool.wait_ge(sta_hi_done, nth(SPLITS, c, name) + 1)
                nc.gpsimd.tensor_tensor(tiles(sta_lo[i][:, :]), val[:, :, :],
                                        tiles(sta_hi[i][:, :]).bitcast(F32), ALU.subtract)\
                    .then_inc(sta_lo_done, 1)

            def cycle(c):
                last_job = before(c, lambda k: sum(0 <= k - lag < B for _, lag in JOBS))
                for s in range(SLOTS):
                    if (ahead := at(c, s + LO_AHEAD)) and not lo_on_dve(ahead[1]):
                        low_part(*ahead)
                    if s == 0 and c.has(1):
                        power(last_job)
                        sta_low(c, 1, "B")
                    if s == 6 and c.has(0):
                        power(nth(JOBS, c, "E") + 1)
                    if s == 8 and c.has(0):
                        sta_low(c, 0, "E")
                    if s == 12 and c.has(2):
                        power(nth(JOBS, c, "D") + 1)
                    if s == 16 and c.has(2):
                        sta_low(c, 1, "D")
                    if s == 19 and c.has(1):
                        power(nth(JOBS, c, "A") + 1)
                    if s == 24 and c.has(1):
                        sta_low(c, 0, "A")
                    if s == 27 and c.has(0):
                        power(nth(JOBS, c, "Bn") + 1)

            nc.gpsimd.memset(expo[:, :], -0.5).then_inc(expo_set, 1)
            pool.wait_ge(expo_set, 1)
            run(pool, cycle)


def kernel(x, adj, L0_gnn_W, L0_gnn_b, L1_gnn_W0, L1_gnn_b0, L1_gnn_W1, L1_gnn_b1, L1_gnn_W2, L1_gnn_b2):
    import numpy as np
    import concourse.bacc as bacc
    from concourse.bass_utils import run_bass_kernel_spmd

    nc = bacc.Bacc("TRN2", target_bir_lowering=False, num_devices=1)
    x, adj, W = np.asarray(x), np.asarray(adj), np.asarray(L0_gnn_W)
    D = x.shape[2]
    consts = np.concatenate(
        [np.asarray(L1_gnn_W0), np.asarray(L1_gnn_W1), np.asarray(L1_gnn_W2), W[:, :D].T, W[:, D:].T]
        + [np.repeat(np.asarray(b)[None, :], P, axis=0) for b in (L1_gnn_b0, L1_gnn_b1, L1_gnn_b2, L0_gnn_b)]
        + [np.eye(P, dtype=np.float32)], axis=1)
    arrays = {
        "in_x": np.ascontiguousarray(x),
        "in_adj": np.ascontiguousarray(adj),
        "in_adj_t": np.ascontiguousarray(adj.transpose(0, 2, 1)),
        "in_consts": np.ascontiguousarray(consts),
    }
    args = [nc.dram_tensor(n, a.shape, mybir.dt.from_np(a.dtype), kind="ExternalInput").ap()
            for n, a in arrays.items()]
    out = nc.dram_tensor("out", x.shape, F32, kind="ExternalOutput").ap()
    build(nc, *args, out)
    r = run_bass_kernel_spmd(nc, [arrays], core_ids=[0])
    return r.results[0]["out"]
```

```python
from contextlib import ExitStack

import concourse.bass as bass
from concourse import mybir

ALU = mybir.AluOpType
ACT = mybir.ActivationFunctionType
F32 = mybir.dt.float32
F32R = mybir.dt.float32r
AX = mybir.AxisListType.X

P = 128
SLOTS = 32
HI_AHEAD, LO_AHEAD, COS_AHEAD = 2, 1, 4
RING = 4
PHASE_AT = {2: 0, 1: 8, 0: 16, 3: 24}
LAG = {2: 2, 1: 1, 0: 0, 3: 2}
LN_EPS = 1e-5
NORM_EPS = 1e-12


def build(nc, x, adj, adj_t, consts, out):
    B, N, D = x.shape
    NT = N // P
    HALF = N // 2
    assert D == P and NT == 8 and SLOTS == 4 * NT and B % 2 == 0 and B > 3
    PAIRS = NT // 2
    LAST = B + 1

    ADJ_SLOT = [0, 1, 2, 3, 4, 5, 0, 1]
    PE_AT = dict(B_nhT=2, E_hT=9, E_e=10, D_H=11, D_nhT=15, A_H=18, A_nhT=26, B_z=23, B_hT=29, B_H=31, C_out=31)
    DVE_AT = dict(B_make=0, B_var=1, B_nrm=2, B_low=4, E_sum=5, E_val=6, E_var=7, E_nrm=8, E_e=11, D_make=13, D_var=13, D_nrm=13, D_low=16, A_make=18, A_var=21, A_nrm=24, A_low=28, B_z=25, B_x1=26, B_val=27, B_var1=28, B_nrm1=29, C_out=31)
    ACT_AT = dict(B_sq=0, B_root=1, B_sta=0, B_high=2, E_sq=6, E_root=7, E_h=8, E_hT=10, D_sq=13, D_root=13, D_sta=14, D_high=16, A_sq=21, A_root=22, A_sta=25, A_high=27, B_sq1=27, B_root1=27, B_hT=30)
    POOL_AT = dict(B=3, E=10, D=17, A=27)

    class Cycle:
        def __init__(self, k, i=None):
            self.k, self.i = k, i

        def graph(self, lag):
            return self.k - lag + (0 if self.i is None else 2 * self.i)

        def has(self, lag):
            return 0 <= self.k - lag < B

        def next(self):
            return Cycle(self.k + 1, self.i)

    def phase_of(slot):
        return next(f for f in PHASE_AT if PHASE_AT[f] <= slot < PHASE_AT[f] + NT)

    def active(k):
        return [s for s in range(SLOTS) if 0 <= k - LAG[phase_of(s)] < B]

    def before(c, per_cycle):
        n = sum(per_cycle(k) for k in range(c.k))
        return n if c.i is None else n + 2 * per_cycle(3) * c.i

    def item(c, s):
        return before(c, lambda k: len(active(k))) + active(c.k).index(s)

    def is_cos(s):
        return phase_of(s) != 0

    def cos_item(c, s):
        return (before(c, lambda k: sum(map(is_cos, active(k))))
                + sum(is_cos(t) for t in active(c.k) if t < s))

    LO_ON_DVE = {1, 4, 7, 11, 12, 16, 17, 18, 21, 22, 23, 24, 31}

    def lo_on_dve(s):
        return s in LO_ON_DVE

    def lows(c, s, dve):
        return (before(c, lambda k: sum(lo_on_dve(t) == dve for t in active(k)))
                + sum(lo_on_dve(t) == dve for t in active(c.k) if t < s))

    def wait_low(eng, c, s):
        dve = lo_on_dve(s)
        eng.wait_ge(lo_sem[dve], lows(c, s, dve) + 1)

    def phases_before(c, f):
        return (before(c, lambda k: len(active(k)) // NT)
                + sum(c.has(LAG[g]) for g in PHASE_AT if PHASE_AT[g] < PHASE_AT[f]))

    JOBS = [("E", 0), ("D", 2), ("A", 1)]
    SPLITS = [("B", 1), ("E", 0), ("D", 2), ("A", 1)]
    NHTS = [("B", 1), ("D", 2), ("A", 1)]
    STAGES = [("B_nhT", 1), ("E_hT", 0), ("E_e", 0), ("D_H", 2), ("D_nhT", 2), ("A_H", 1),
              ("B_z", 0), ("A_nhT", 1), ("B_hT", 0), ("C_out", 2), ("B_H", 0)]

    def nth(events, c, name):
        n = before(c, lambda k: sum(0 <= k - lag < B for _, lag in events))
        for e, lag in events:
            if e == name:
                return n
            n = n + int(c.has(lag))
        return n

    ctx = ExitStack()
    with ctx:
        def sb(name, shape, dt=F32):
            return ctx.enter_context(nc.sbuf_tensor(name, shape, dt))

        def sem(name):
            return ctx.enter_context(nc.semaphore(name))

        adj_sb = sb("adj_sb", [P, max(ADJ_SLOT) + 1, N])
        adjt_sb = [sb(f"adjt_sb{p}", [P, NT, N]) for p in range(2)]
        ew = sb("ew", [P, 2, N])
        mov_hi = sb("mov_hi", [P, RING, N], F32R)
        mov_lo = sb("mov_lo", [P, RING, N], F32R)
        sta_hi = [sb(f"sta_hi{i}", [P, N], F32R) for i in range(2)]
        sta_lo = [sb(f"sta_lo{i}", [P, N], F32R) for i in range(2)]
        nht_hi = [sb(f"nht_hi{i}", [P, N], F32R) for i in range(2)]
        nht_lo = [sb(f"nht_lo{i}", [P, N], F32R) for i in range(2)]
        x_sb = sb("x_sb", [P, NT, D])
        x1_sb = sb("x1_sb", [P, NT, D])
        park = [sb(f"park{p}", [P, NT, D]) for p in range(2)]
        yt = sb("yt", [P, N])
        val = [sb(f"val{i}", [P, NT, D]) for i in range(2)]
        scr = [sb(f"scr{i}", [P, NT, D]) for i in range(2)]
        e_sb = sb("e_sb", [P, NT, D])
        cst = sb("cst", [P, consts.shape[1]])
        deg = sb("deg", [P, NT])
        rdeg = sb("rdeg", [P, NT])
        rsum, ssum, var, root, inv, est, rstd = (
            [sb(f"{name}{i}", [P, NT]) for i in range(2)]
            for name in ("rsum", "ssum", "var", "root", "inv", "est", "rstd"))

        w = [cst[:, i * D:(i + 1) * D] for i in range(3)]
        wa_t, wb_t = cst[:, 3 * D:4 * D], cst[:, 4 * D:5 * D]
        bias = [cst[:, (5 + i) * D:(6 + i) * D].unsqueeze(1).to_broadcast([P, NT, D]) for i in range(3)]
        bias_l0 = cst[:, 8 * D:9 * D].unsqueeze(1).to_broadcast([P, NT, D])
        ident = cst[:, 9 * D:10 * D]

        gram = ctx.enter_context(nc.psum_tensor("gram", [P, 2, N], F32))
        ysum = ctx.enter_context(nc.psum_tensor("ysum", [P, N], F32))
        stage = ctx.enter_context(nc.psum_tensor("stage", [P, NT, D], F32))

        const_in = sem("const_in")
        x_in = sem("x_in")
        adj_in = [sem(f"adj_in{g}") for g in range(PAIRS)]
        adjt_in = [[sem(f"adjt_in{p}_{g}") for g in range(PAIRS)] for p in range(2)]
        parked = sem("parked")
        out_done = sem("out_done")
        cos_done = sem("cos_done")
        ew_done = sem("ew_done")
        hi_done = sem("hi_done")
        lo_dve = sem("lo_dve")
        lo_pool = sem("lo_pool")
        lo_sem = {True: lo_dve, False: lo_pool}
        hi_summed = sem("hi_summed")
        item_done = sem("item_done")
        y_read = sem("y_read")
        stage_full = sem("stage_full")
        stage_read = sem("stage_read")
        def by_set(name):
            return [sem(f"{name}{i}") for i in range(2)]

        rsum_done = by_set("rsum_done")
        centred = by_set("centred")
        sq_done = by_set("sq_done")
        ss_done = by_set("ss_done")
        var_done = by_set("var_done")
        root_done = by_set("root_done")
        newton = by_set("newton")
        nrm_done = by_set("nrm_done")
        sta_hi_done = sem("sta_hi_done")
        sta_lo_done = sem("sta_lo_done")
        nht_hi_done = sem("nht_hi_done")
        h_done = sem("h_done")
        rdeg_done = sem("rdeg_done")
        ze_done = sem("ze_done")
        x1_done = sem("x1_done")

        def tiles(ap):
            return ap.rearrange("p (t d) -> p t d", t=NT)

        def flat(buf):
            return buf[:, :, :].rearrange("p t d -> p (t d)")

        def rows(dram, b):
            return dram[b].rearrange("(t p) d -> p t d", p=P)

        def run(eng, cycle):
            for k in (0, 1):
                cycle(Cycle(k))
            with eng.Fori(0, (B - 2) // 2) as i:
                for k in (2, 3):
                    cycle(Cycle(k, i))
            for k in range(B, LAST + 1):
                cycle(Cycle(k))

        def at(c, s):
            c, s = (c, s) if s < SLOTS else (c.next(), s - SLOTS)
            return (c, s) if s in active(c.k) else None

        block = ctx.enter_context(nc.Block())

        @block.sync
        def _(sp):
            sp.dma_start(cst[:, :], consts[:, :]).then_inc(const_in, 16)

            def cycle(c):
                if c.has(0):
                    b = c.graph(0)
                    if c.k > 0:
                        sp.wait_ge(x1_done, b)
                    sp.dma_start(x_sb[:, :, :], rows(x, b)).then_inc(x_in, 16)
                    if c.k > 0:
                        sp.wait_ge(item_done, item_end(c))
                    for g in range(PAIRS):
                        first = ADJ_SLOT[2 * g]
                        if first in ADJ_SLOT[:2 * g]:
                            at_slot = PHASE_AT[0] + ADJ_SLOT.index(first) + 1
                            sp.wait_ge(lo_dve, lows(c, at_slot, True) + 1)
                        sp.dma_start(adj_sb[:, first:first + 2, :],
                                     rows(adj, b)[:, 2 * g:2 * g + 2, :]).then_inc(adj_in[g], 16)
                    for g in range(PAIRS):
                        if c.has(2):
                            sp.wait_ge(ew_done, cos_item(c, PHASE_AT[3] + 2 * g + 1) + 1)
                        sp.dma_start(adjt_sb[c.k % 2][:, 2 * g:2 * g + 2, :],
                                     rows(adj_t, b)[:, 2 * g:2 * g + 2, :]).then_inc(adjt_in[c.k % 2][g], 16)
                if c.has(2):
                    sp.wait_ge(stage_read, nth(STAGES, c, "C_out") + 1)
                    sp.dma_start(rows(out, c.graph(2)), park[c.k % 2][:, :, :]).then_inc(out_done, 16)
                if c.has(0):
                    if c.has(2):
                        sp.wait_ge(out_done, 16 * (c.graph(2) + 1))
                    else:
                        sp.wait_ge(x1_done, c.graph(0) + 1)
                    sp.dma_start(park[c.k % 2][:, :, :], x1_sb[:, :, :]).then_inc(parked, 16)

            def item_end(c):
                return before(c, lambda k: len(active(k)))

            run(sp, cycle)
            sp.wait_ge(out_done, 16 * B)

        @block.tensor
        def _(pe):
            def cosines(now, c, s):
                q, f = s % NT, phase_of(s)
                hi, lo = nht_hi[f % 2], nht_lo[f % 2]
                n = cos_item(c, s)
                if q == 0:
                    made = {2: "A_nhT", 1: "B_nhT", 3: "D_nhT"}[f]
                    pe.wait_ge(stage_read, nth(STAGES, now if f == 2 else c, made) + 1)
                if not (c.i is None and n < 2):
                    pe.wait_ge(ew_done, n - 1)
                cols = slice(q * P, (q + 1) * P)
                for sta, mov, first, last in ((lo, hi, True, False), (hi, lo, False, False), (hi, hi, False, True)):
                    for h in range(2):
                        part = slice(h * HALF, (h + 1) * HALF)
                        mm = nc.tensor.matmul(gram[:, q % 2, part], sta[:, cols], mov[:, part],
                                              start=first, stop=last)
                mm.then_inc(cos_done, 1)

            def sum_high(c, s):
                q, f = s % NT, phase_of(s)
                if q == 0:
                    n = {2: nth(SPLITS, c, "B"), 1: nth(SPLITS, c, "B") + 1,
                         0: nth(SPLITS, c, "E") + 1, 3: nth(SPLITS, c, "D") + 1}[f]
                    pe.wait_ge(sta_hi_done, n)
                    pe.wait_ge(sta_lo_done, n)
                    if not (c.i is None and phases_before(c, f) == 0):
                        pe.wait_ge(y_read, phases_before(c, f))
                pe.wait_ge(hi_done, item(c, s) + 1)
                for sta in (sta_hi[f % 2], sta_lo[f % 2]):
                    for h in range(2):
                        part = slice(h * HALF, (h + 1) * HALF)
                        mm = nc.tensor.matmul(ysum[:, part], sta[:, q * P:(q + 1) * P],
                                              mov_hi[:, q % RING, part],
                                              start=(q == 0 and sta is sta_hi[f % 2]), stop=False)
                mm.then_inc(hi_summed, 1)

            def sum_low(c, s):
                q, f = s % NT, phase_of(s)
                wait_low(pe, c, s)
                for h in range(2):
                    part = slice(h * HALF, (h + 1) * HALF)
                    mm = nc.tensor.matmul(ysum[:, part], sta_hi[f % 2][:, q * P:(q + 1) * P],
                                          mov_lo[:, q % RING, part], start=False, stop=(q == NT - 1))
                mm.then_inc(item_done, 1)

            def stage_free(c, name):
                n = nth(STAGES, c, name)
                if not (c.i is None and n == 0):
                    pe.wait_ge(stage_read, n)

            def rows_times(ft, weights):
                for t in range(NT):
                    mm = nc.tensor.matmul(stage[:, t, :], ft[:, t * P:(t + 1) * P], weights,
                                          start=True, stop=True)
                mm.then_inc(stage_full, 1)

            def transposes(src):
                for t in range(NT):
                    mm = nc.tensor.transpose(stage[:, t, :], src(t), ident)
                mm.then_inc(stage_full, 1)

            def cycle(c):
                for s in range(SLOTS):
                    if at(c, s):
                        sum_high(c, s)
                        if s % NT > 0:
                            sum_low(c, s - 1)
                        if s % NT == NT - 1:
                            sum_low(c, s)
                    if (ahead := at(c, s + COS_AHEAD)) and is_cos(ahead[1]):
                        cosines(c, *ahead)
                    if s == PE_AT["B_nhT"] and c.has(1):
                        stage_free(c, "B_nhT")
                        pe.wait_ge(nrm_done[1], 2 * c.graph(1) + 2)
                        transposes(lambda t: scr[1][:, t, :])
                    if s == PE_AT["E_hT"] and c.has(0):
                        stage_free(c, "E_hT")
                        pe.wait_ge(h_done, c.graph(0) + 1)
                        transposes(lambda t: val[0][:, t, :])
                    if s == PE_AT["E_e"] and c.has(0):
                        stage_free(c, "E_e")
                        rows_times(flat(e_sb), wa_t)
                    if s == PE_AT["D_H"] and c.has(2):
                        stage_free(c, "D_H")
                        pe.wait_ge(y_read, phases_before(c, 1))
                        rows_times(yt[:, :], w[2])
                    if s == PE_AT["D_nhT"] and c.has(2):
                        stage_free(c, "D_nhT")
                        pe.wait_ge(nrm_done[0], nth(JOBS, c, "D") + 1)
                        transposes(lambda t: scr[0][:, t, :])
                    if s == PE_AT["A_H"] and c.has(1):
                        stage_free(c, "A_H")
                        pe.wait_ge(y_read, phases_before(c, 0))
                        rows_times(yt[:, :], w[1])
                    if s == PE_AT["B_z"] and c.has(0):
                        stage_free(c, "B_z")
                        pe.wait_ge(y_read, phases_before(c, 3))
                        rows_times(yt[:, :], wb_t)
                    if s == PE_AT["A_nhT"] and c.has(1):
                        stage_free(c, "A_nhT")
                        pe.wait_ge(nrm_done[0], nth(JOBS, c, "A") + 1)
                        transposes(lambda t: scr[0][:, t, :])
                    if s == PE_AT["B_hT"] and c.has(0):
                        stage_free(c, "B_hT")
                        pe.wait_ge(nrm_done[1], 2 * c.graph(0) + 1)
                        transposes(lambda t: scr[1][:, t, :])
                    if s == PE_AT["C_out"] and c.has(2):
                        stage_free(c, "C_out")
                        pe.wait_ge(y_read, phases_before(c, 3) + 1)
                        transposes(lambda t: yt[:, t * P:(t + 1) * P])
                    if s == PE_AT["B_H"] and c.has(0):
                        stage_free(c, "B_H")
                        rows_times(flat(e_sb), w[0])

            pe.wait_ge(const_in, 16)
            run(pe, cycle)

        @block.vector
        def _(dve):
            def times_adj(c, s):
                q, f = s % NT, phase_of(s)
                parity = (c.k - LAG[f]) % 2
                if f == 1 and q % 2 == 0:
                    dve.wait_ge(adjt_in[parity][q // 2],
                                16 * ((c.k - 1) // 2 + 1 + (0 if c.i is None else c.i)))
                dve.wait_ge(cos_done, cos_item(c, s) + 1)
                before_s = [t for t in active(c.k) if is_cos(t) and t < s]
                if len(before_s) >= 2:
                    wait_low(dve, c, before_s[-2])
                elif not (c.i is None and cos_item(c, s) < 2):
                    for on_dve, done in ((False, lo_pool), (True, lo_dve)):
                        of_last = 0 if before_s else int(lo_on_dve(SLOTS - 1) == on_dve)
                        dve.wait_ge(done, lows(c, 0, on_dve) - of_last)
                nc.vector.tensor_tensor(ew[:, q % 2, :], adjt_sb[parity][:, q, :], gram[:, q % 2, :],
                                        ALU.mult).then_inc(ew_done, 1)

            def low_part(c, s):
                q = s % NT
                n = item(c, s)
                dve.wait_ge(hi_done, n + 1)
                if not (c.i is None and n < RING):
                    dve.wait_ge(item_done, n - RING + 1)
                src = ew[:, q % 2, :] if is_cos(s) else adj_sb[:, ADJ_SLOT[q], :]
                nc.vector.tensor_tensor(mov_lo[:, q % RING, :], src, mov_hi[:, q % RING, :].bitcast(F32),
                                        ALU.subtract).then_inc(lo_dve, 1)

            def bc(ap):
                return ap.unsqueeze(2).to_broadcast([P, NT, D])

            def val_free(c, splits):
                if not (c.i is None and splits == 0):
                    dve.wait_ge(sta_hi_done, splits)
                    dve.wait_ge(sta_lo_done, splits)

            def row_sums(i, n, src):
                nc.vector.tensor_reduce(rsum[i][:, :], src[:, :, :], AX, ALU.add).then_inc(rsum_done[i], 1)

            def centre(i, n, src):
                dve.wait_ge(rsum_done[i], n)
                nc.vector.scalar_tensor_tensor(out=val[i][:, :, :], in0=bc(rsum[i][:, :]), scalar=-1.0 / D,
                                               in1=src[:, :, :], op0=ALU.mult, op1=ALU.add)\
                    .then_inc(centred[i], 1)

            def variance(i, n, layernorm):
                dve.wait_ge(sq_done[i], n)
                nc.vector.tensor_reduce(ssum[i][:, :], scr[i][:, :, :], AX, ALU.add).then_inc(ss_done[i], 1)
                dve.wait_ge(ss_done[i], n)
                if layernorm:
                    nc.vector.tensor_scalar(var[i][:, :], ssum[i][:, :], 1.0 / D, LN_EPS, ALU.mult,
                                            ALU.add).then_inc(var_done[i], 1)
                else:
                    nc.vector.tensor_scalar(var[i][:, :], ssum[i][:, :], NORM_EPS * NORM_EPS, None,
                                            ALU.max).then_inc(var_done[i], 1)

            def normalise(i, n):
                dve.wait_ge(root_done[i], n)
                nc.vector.reciprocal(inv[i][:, :], root[i][:, :]).then_inc(newton[i], 1)
                dve.wait_ge(newton[i], 4 * n - 3)
                nc.vector.tensor_tensor(est[i][:, :], inv[i][:, :], var[i][:, :], ALU.mult).then_inc(newton[i], 1)
                dve.wait_ge(newton[i], 4 * n - 2)
                nc.vector.tensor_tensor(inv[i][:, :], est[i][:, :], root[i][:, :], ALU.add).then_inc(newton[i], 1)
                dve.wait_ge(newton[i], 4 * n - 1)
                nc.vector.reciprocal(rstd[i][:, :], inv[i][:, :]).then_inc(newton[i], 1)
                dve.wait_ge(newton[i], 4 * n)
                nc.vector.scalar_tensor_tensor(out=scr[i][:, :, :], in0=val[i][:, :, :], scalar=2.0,
                                               in1=bc(rstd[i][:, :]), op0=ALU.mult, op1=ALU.mult)\
                    .then_inc(nrm_done[i], 1)

            def make_h(c, stage_name, i, b):
                dve.wait_ge(stage_full, nth(STAGES, c, stage_name) + 1)
                nc.vector.tensor_tensor(val[i][:, :, :], stage[:, :, :], b, ALU.add).then_inc(stage_read, 1)

            def nht_low(c, stage_name, name, i):
                dve.wait_ge(nht_hi_done, nth(NHTS, c, name) + 1)
                nc.vector.tensor_tensor(tiles(nht_lo[i][:, :]), stage[:, :, :],
                                        tiles(nht_hi[i][:, :]).bitcast(F32), ALU.subtract)\
                    .then_inc(stage_read, 1)

            def cycle(c):
                for s in range(SLOTS):
                    if (ahead := at(c, s + HI_AHEAD)) and is_cos(ahead[1]):
                        times_adj(*ahead)
                    if (ahead := at(c, s + LO_AHEAD)) and lo_on_dve(ahead[1]):
                        low_part(*ahead)
                    if s == DVE_AT["B_make"] and c.has(1):
                        n = prior_stages(c)
                        dve.wait_ge(stage_full, n)
                        nc.vector.tensor_tensor(val[1][:, :, :], stage[:, :, :], bias[0],
                                                ALU.add).then_inc(stage_read, 1)
                    if s == DVE_AT["B_var"] and c.has(1):
                        variance(1, 2 * c.graph(1) + 2, False)
                    if s == DVE_AT["B_nrm"] and c.has(1):
                        normalise(1, 2 * c.graph(1) + 2)
                    if s == DVE_AT["B_low"] and c.has(1):
                        nht_low(c, "B_nhT", "B", 1)
                    if s == DVE_AT["E_sum"] and c.has(0):
                        dve.wait_ge(x_in, 16 * (c.graph(0) + 1))
                        row_sums(0, c.graph(0) + 1, x_sb)
                    if s == DVE_AT["E_val"] and c.has(0):
                        val_free(c, nth(SPLITS, c, "E"))
                        centre(0, c.graph(0) + 1, x_sb)
                    if s == DVE_AT["E_var"] and c.has(0):
                        variance(0, nth(JOBS, c, "E") + 1, True)
                    if s == DVE_AT["E_nrm"] and c.has(0):
                        normalise(0, nth(JOBS, c, "E") + 1)
                    if s == DVE_AT["E_e"] and c.has(0):
                        dve.wait_ge(stage_full, nth(STAGES, c, "E_e") + 1)
                        nc.vector.tensor_tensor(e_sb[:, :, :], stage[:, :, :], bias_l0,
                                                ALU.add).then_inc(stage_read, 1)
                    if s == DVE_AT["D_make"] and c.has(2):
                        val_free(c, nth(SPLITS, c, "D"))
                        make_h(c, "D_H", 0, bias[2])
                    if s == DVE_AT["D_var"] and c.has(2):
                        variance(0, nth(JOBS, c, "D") + 1, False)
                    if s == DVE_AT["D_nrm"] and c.has(2):
                        normalise(0, nth(JOBS, c, "D") + 1)
                    if s == DVE_AT["D_low"] and c.has(2):
                        nht_low(c, "D_nhT", "D", 1)
                    if s == DVE_AT["A_make"] and c.has(1):
                        val_free(c, nth(SPLITS, c, "A"))
                        make_h(c, "A_H", 0, bias[1])
                    if s == DVE_AT["A_var"] and c.has(1):
                        variance(0, nth(JOBS, c, "A") + 1, False)
                    if s == DVE_AT["A_nrm"] and c.has(1):
                        normalise(0, nth(JOBS, c, "A") + 1)
                    if s == DVE_AT["A_low"] and c.has(1):
                        nht_low(c, "A_nhT", "A", 0)
                    if s == DVE_AT["B_z"] and c.has(0):
                        b = c.graph(0)
                        dve.wait_ge(y_read, phases_before(c, 3))
                        nc.vector.reciprocal(rdeg[:, :], deg[:, :]).then_inc(rdeg_done, 1)
                        dve.wait_ge(rdeg_done, b + 1)
                        dve.wait_ge(stage_full, nth(STAGES, c, "B_z") + 1)
                        nc.vector.tensor_tensor(scr[1][:, :, :], stage[:, :, :], bc(rdeg[:, :]), ALU.mult)\
                            .then_inc(stage_read, 1)
                        dve.wait_ge(stage_read, nth(STAGES, c, "B_z") + 1)
                        nc.vector.tensor_tensor(scr[1][:, :, :], scr[1][:, :, :], e_sb[:, :, :],
                                                ALU.add).then_inc(ze_done, 1)
                    if s == DVE_AT["B_x1"] and c.has(0):
                        b = c.graph(0)
                        dve.wait_ge(ze_done, b + 1)
                        if c.k > 0:
                            dve.wait_ge(parked, 16 * b)
                        nc.vector.scalar_tensor_tensor(out=x1_sb[:, :, :], in0=scr[1][:, :, :], scalar=0.0,
                                                       in1=x_sb[:, :, :], op0=ALU.max,
                                                       op1=ALU.add).then_inc(x1_done, 1)
                        dve.wait_ge(x1_done, b + 1)
                        row_sums(1, b + 1, x1_sb)
                    if s == DVE_AT["B_val"] and c.has(0):
                        if c.has(1):
                            val_free(c, nth(SPLITS, c, "B") + 1)
                        centre(1, c.graph(0) + 1, x1_sb)
                    if s == DVE_AT["B_var1"] and c.has(0):
                        variance(1, 2 * c.graph(0) + 1, True)
                    if s == DVE_AT["B_nrm1"] and c.has(0):
                        normalise(1, 2 * c.graph(0) + 1)
                    if s == DVE_AT["C_out"] and c.has(2):
                        b = c.graph(2)
                        dve.wait_ge(parked, 16 * (b + 1))
                        dve.wait_ge(stage_full, nth(STAGES, c, "C_out") + 1)
                        nc.vector.tensor_tensor(park[c.k % 2][:, :, :], stage[:, :, :],
                                                park[c.k % 2][:, :, :], ALU.add)\
                            .then_inc(stage_read, 1)

            def prior_stages(c):
                return before(c, lambda k: sum(0 <= k - lag < B for _, lag in STAGES))

            dve.wait_ge(const_in, 16)
            run(dve, cycle)

        @block.scalar
        def _(act):
            def high_part(c, s):
                q, n = s % NT, item(c, s)
                if is_cos(s):
                    act.wait_ge(ew_done, cos_item(c, s) + 1)
                    src = ew[:, q % 2, :]
                else:
                    if q % 2 == 0:
                        act.wait_ge(adj_in[q // 2], 16 * (c.graph(0) + 1))
                    src = adj_sb[:, ADJ_SLOT[q], :]
                if not (c.i is None and n < RING):
                    act.wait_ge(hi_summed, n - RING + 1)
                    pos = active(c.k).index(s)
                    old = active(c.k)[pos - RING] if pos >= RING else None
                    if c.k == 1 and pos < RING:
                        wait_low(act, Cycle(0), active(0)[pos - RING])
                    elif old is not None and not (is_cos(s) and is_cos(old)):
                        wait_low(act, c, old)
                if is_cos(s):
                    nc.scalar.activation(mov_hi[:, q % RING, :], src, ACT.Copy).then_inc(hi_done, 1)
                else:
                    nc.scalar.activation(mov_hi[:, q % RING, :], src, ACT.Identity,
                                         accum_out=deg[:, q:q + 1]).then_inc(hi_done, 1)

            def read_sum(c, f):
                s = PHASE_AT[f] + NT - 1
                act.wait_ge(item_done, item(c, s) + 1)
                prior = {2: "E_hT", 1: "A_H", 0: "B_z", 3: "C_out"}[f]
                n = nth(STAGES, c, prior)
                if not (c.i is None and n == 0):
                    act.wait_ge(stage_full, n)
                nc.scalar.activation(yt[:, :], ysum[:, :], ACT.Relu if f in (1, 2) else ACT.Copy)\
                    .then_inc(y_read, 1)

            def squares(i, read):
                if read is not None:
                    act.wait_ge(stage_full, read)
                nc.scalar.activation(scr[i][:, :, :], val[i][:, :, :], ACT.Square).then_inc(sq_done[i], 1)

            def square_root(i, n):
                act.wait_ge(var_done[i], n)
                nc.scalar.activation(root[i][:, :], var[i][:, :], ACT.Sqrt).then_inc(root_done[i], 1)

            def sta_high(i, v, n):
                if n is not None:
                    act.wait_ge(item_done, n)
                nc.scalar.activation(tiles(sta_hi[i][:, :]), val[v][:, :, :], ACT.Copy).then_inc(sta_hi_done, 1)

            def nht_high(c, stage_name, i):
                act.wait_ge(stage_full, nth(STAGES, c, stage_name) + 1)
                nc.scalar.activation(tiles(nht_hi[i][:, :]), stage[:, :, :], ACT.Copy).then_inc(nht_hi_done, 1)

            def cycle(c):
                for s in range(SLOTS):
                    if ahead := at(c, s + HI_AHEAD):
                        high_part(*ahead)
                    if s == NT - 1 and c.has(2):
                        read_sum(c, 2)
                    if s == 2 * NT - 1 and c.has(1):
                        read_sum(c, 1)
                    if s == 3 * NT - 1 and c.has(0):
                        read_sum(c, 0)
                    if s == 4 * NT - 1 and c.has(2):
                        read_sum(c, 3)
                    if s == ACT_AT["B_sq"] and c.has(1):
                        n = before(c, lambda k: sum(0 <= k - lag < B for _, lag in STAGES))
                        act.wait_ge(stage_read, n)
                        squares(1, None)
                    if s == ACT_AT["B_root"] and c.has(1):
                        square_root(1, 2 * c.graph(1) + 2)
                    if s == ACT_AT["B_sta"] and c.has(1):
                        sta_high(1, 1, items_before(c))
                    if s == ACT_AT["B_high"] and c.has(1):
                        nht_high(c, "B_nhT", 1)
                    if s == ACT_AT["E_sq"] and c.has(0):
                        act.wait_ge(centred[0], c.graph(0) + 1)
                        squares(0, nth(STAGES, c, "E_hT") if c.k > 0 else None)
                    if s == ACT_AT["E_root"] and c.has(0):
                        square_root(0, nth(JOBS, c, "E") + 1)
                    if s == ACT_AT["E_h"] and c.has(0):
                        act.wait_ge(nrm_done[0], nth(JOBS, c, "E") + 1)
                        nc.scalar.activation(val[0][:, :, :], scr[0][:, :, :], ACT.Relu).then_inc(h_done, 1)
                        act.wait_ge(h_done, c.graph(0) + 1)
                        sta_high(0, 0, item(c, 7) + 1 if c.has(2) else items_before(c) if c.k > 0 else None)
                    if s == ACT_AT["E_hT"] and c.has(0):
                        act.wait_ge(stage_full, nth(STAGES, c, "E_hT") + 1)
                        nc.scalar.activation(e_sb[:, :, :], stage[:, :, :], ACT.Copy).then_inc(stage_read, 1)
                    if s == ACT_AT["D_sq"] and c.has(2):
                        act.wait_ge(stage_read, nth(STAGES, c, "D_H") + 1)
                        squares(0, nth(STAGES, c, "D_H"))
                    if s == ACT_AT["D_root"] and c.has(2):
                        square_root(0, nth(JOBS, c, "D") + 1)
                    if s == ACT_AT["D_sta"] and c.has(2):
                        sta_high(1, 0, item(c, 15) + 1 if c.has(1) else item(c, 7) + 1)
                    if s == ACT_AT["D_high"] and c.has(2):
                        nht_high(c, "D_nhT", 1)
                    if s == ACT_AT["A_sq"] and c.has(1):
                        act.wait_ge(stage_read, nth(STAGES, c, "A_H") + 1)
                        squares(0, nth(STAGES, c, "A_H"))
                    if s == ACT_AT["A_root"] and c.has(1):
                        square_root(0, nth(JOBS, c, "A") + 1)
                    if s == ACT_AT["A_sta"] and c.has(1):
                        sta_high(0, 0, item(c, 23) + 1 if c.has(0) else item(c, 15) + 1)
                    if s == ACT_AT["A_high"] and c.has(1):
                        nht_high(c, "A_nhT", 0)
                    if s == ACT_AT["B_sq1"] and c.has(0):
                        act.wait_ge(centred[1], c.graph(0) + 1)
                        squares(1, nth(STAGES, c, "B_z"))
                    if s == ACT_AT["B_root1"] and c.has(0):
                        square_root(1, 2 * c.graph(0) + 1)
                    if s == ACT_AT["B_hT"] and c.has(0):
                        act.wait_ge(stage_full, nth(STAGES, c, "B_hT") + 1)
                        nc.scalar.activation(e_sb[:, :, :], stage[:, :, :], ACT.Relu).then_inc(stage_read, 1)

            def items_before(c):
                return before(c, lambda k: len(active(k)))

            run(act, cycle)

        @block.gpsimd
        def _(pool):
            def low_part(c, s):
                q, n = s % NT, item(c, s)
                pool.wait_ge(hi_done, n + 1)
                if not (c.i is None and n < RING):
                    pool.wait_ge(item_done, n - RING + 1)
                src = ew[:, q % 2, :] if is_cos(s) else adj_sb[:, ADJ_SLOT[q], :]
                nc.gpsimd.tensor_tensor(mov_lo[:, q % RING, :], src, mov_hi[:, q % RING, :].bitcast(F32),
                                        ALU.subtract).then_inc(lo_pool, 1)

            def sta_low(c, i, name):
                v = 1 if name == "B" else 0
                pool.wait_ge(sta_hi_done, nth(SPLITS, c, name) + 1)
                nc.gpsimd.tensor_tensor(tiles(sta_lo[i][:, :]), val[v][:, :, :],
                                        tiles(sta_hi[i][:, :]).bitcast(F32), ALU.subtract)\
                    .then_inc(sta_lo_done, 1)

            def cycle(c):
                for s in range(SLOTS):
                    if (ahead := at(c, s + LO_AHEAD)) and not lo_on_dve(ahead[1]):
                        low_part(*ahead)
                    if s == POOL_AT["B"] and c.has(1):
                        sta_low(c, 1, "B")
                    if s == POOL_AT["E"] and c.has(0):
                        sta_low(c, 0, "E")
                    if s == POOL_AT["D"] and c.has(2):
                        sta_low(c, 1, "D")
                    if s == POOL_AT["A"] and c.has(1):
                        sta_low(c, 0, "A")

            run(pool, cycle)


def kernel(x, adj, L0_gnn_W, L0_gnn_b, L1_gnn_W0, L1_gnn_b0, L1_gnn_W1, L1_gnn_b1, L1_gnn_W2, L1_gnn_b2):
    import numpy as np
    import concourse.bacc as bacc
    from concourse.bass_utils import run_bass_kernel_spmd

    nc = bacc.Bacc("TRN2", target_bir_lowering=False, num_devices=1)
    x, adj, W = np.asarray(x), np.asarray(adj), np.asarray(L0_gnn_W)
    D = x.shape[2]
    consts = np.concatenate(
        [np.asarray(L1_gnn_W0), np.asarray(L1_gnn_W1), np.asarray(L1_gnn_W2), W[:, :D].T, W[:, D:].T]
        + [np.repeat(np.asarray(b)[None, :], P, axis=0) for b in (L1_gnn_b0, L1_gnn_b1, L1_gnn_b2, L0_gnn_b)]
        + [np.eye(P, dtype=np.float32)], axis=1)
    arrays = {
        "in_x": np.ascontiguousarray(x),
        "in_adj": np.ascontiguousarray(adj),
        "in_adj_t": np.ascontiguousarray(adj.transpose(0, 2, 1)),
        "in_consts": np.ascontiguousarray(consts),
    }
    args = [nc.dram_tensor(n, a.shape, mybir.dt.from_np(a.dtype), kind="ExternalInput").ap()
            for n, a in arrays.items()]
    out = nc.dram_tensor("out", x.shape, F32, kind="ExternalOutput").ap()
    build(nc, *args, out)
    r = run_bass_kernel_spmd(nc, [arrays], core_ids=[0])
    return r.results[0]["out"]
```

```python
from contextlib import ExitStack

import concourse.bass as bass
from concourse import mybir

ALU = mybir.AluOpType
ACT = mybir.ActivationFunctionType
F32 = mybir.dt.float32
F32R = mybir.dt.float32r
AX = mybir.AxisListType.X

P = 128
SLOTS = 32
HI_AHEAD, LO_AHEAD, COS_AHEAD = 2, 1, 4
RING = 4
PHASE_AT = {2: 0, 1: 8, 0: 16, 3: 24}
LAG = {2: 2, 1: 1, 0: 0, 3: 2}
LN_EPS = 1e-5
NORM_EPS = 1e-12


def build(nc, x, adj, adj_t, consts, out):
    B, N, D = x.shape
    NT = N // P
    HALF = N // 2
    assert D == P and NT == 8 and SLOTS == 4 * NT and B % 2 == 0 and B > 3
    PAIRS = NT // 2
    HT = NT // 2
    HALVES = [(h, slice(h * HT, (h + 1) * HT), slice(h * HALF, (h + 1) * HALF)) for h in range(2)]
    LAST = B + 1

    ADJ_SLOT = [0, 1, 2, 3, 4, 5, 0, 1]
    PE_AT = dict(B_nhT=2, E_hT=9, E_e=10, D_H=11, D_nhT=15, A_H=18, A_nhT=25, B_z=23, B_hT=29, B_H=31,
                 C_out=31)
    DVE_AT = dict(B_make=1, B_var=1, B_nrm=2, B_low=4, E_sum=4, E_val=5, E_var=6, E_nrm=8, E_e=12,
                  D_make=13, D_var=14, D_nrm=14, D_low=16, A_make=18, A_var=21, A_nrm=23, A_low=27,
                  B_z=24, B_x1=25, B_val=26, B_var1=28, B_nrm1=29, C_out=31)
    ACT_AT = dict(B_sq=0, B_root=1, B_sta=1, B_high=2, E_sq=5, E_root=6, E_h=8, E_hT=9, D_sq=13,
                  D_root=14, D_sta=16, D_high=16, A_sq=19, A_root=22, A_sta=28, A_high=26, B_sq1=27,
                  B_root1=27, B_hT=29)
    POOL_AT = dict(B=2, E=12, D=14, A=29)

    PE_PEELED = {
        0: dict(E_e=19, B_hT=26, B_z=24),
        1: dict(A_H=17, A_nhT=22, B_z=24, B_hT=30, E_e=9, E_hT=7),
        B: dict(A_nhT=23, A_H=19),
        LAST: dict(D_H=9, D_nhT=14),
    }
    DVE_PEELED = {
        0: dict(E_e=20, B_var1=29, E_val=3, B_val=28, B_nrm1=30, B_z=25, E_sum=3, E_var=7, E_nrm=9),
        1: dict(A_make=17, A_var=19, A_nrm=20, A_low=22, B_x1=28, B_z=23, B_val=28, B_var1=29,
                B_nrm1=30, B_low=5, B_make=2, B_var=3, B_nrm=4, E_var=5, E_nrm=7, E_e=10),
        B: dict(A_make=17, A_var=20),
        LAST: dict(D_make=9, D_var=9, D_nrm=11, D_low=14),
    }
    ACT_PEELED = {
        0: dict(E_h=15, E_hT=16, B_root1=31, B_hT=31, E_root=9),
        1: dict(A_root=20, A_high=21, B_root1=29, B_hT=31, B_sq=1, B_sta=4, B_high=4, A_sta=29,
                E_root=5, E_h=7),
        B: dict(A_sta=22, A_root=19, A_high=24, B_sq=1, A_sq=17, D_sta=15),
        LAST: dict(D_root=11, D_high=11, D_sq=11, D_sta=12),
    }
    POOL_PEELED = {
        1: dict(B=4, E=10, A=30),
        B: dict(B=4, D=18, A=30),
        LAST: dict(D=16),
    }

    class Cycle:
        def __init__(self, k, i=None):
            self.k, self.i = k, i

        def graph(self, lag):
            return self.k - lag + (0 if self.i is None else 2 * self.i)

        def has(self, lag):
            return 0 <= self.k - lag < B

        def next(self):
            return Cycle(self.k + 1, self.i)

    def phase_of(slot):
        return next(f for f in PHASE_AT if PHASE_AT[f] <= slot < PHASE_AT[f] + NT)

    def active(k):
        return [s for s in range(SLOTS) if 0 <= k - LAG[phase_of(s)] < B]

    def before(c, per_cycle):
        n = sum(per_cycle(k) for k in range(c.k))
        return n if c.i is None else n + 2 * per_cycle(3) * c.i

    def item(c, s):
        return before(c, lambda k: len(active(k))) + active(c.k).index(s)

    def is_cos(s):
        return phase_of(s) != 0

    def cos_item(c, s):
        return (before(c, lambda k: sum(map(is_cos, active(k))))
                + sum(is_cos(t) for t in active(c.k) if t < s))

    LO_ON_DVE = {4, 8, 11, 12, 16, 17, 18, 20, 21, 22, 25, 27, 31}
    LO_PEELED = {
        0: {16, 17, 19, 20, 21, 22, 23},
        1: {10, 11, 12, 14, 15, 16, 17, 18, 20, 21, 22},
        B: {6, 8, 10, 12, 29, 31},
        LAST: {0, 2, 5, 7, 24, 28, 31},
    }

    assert all((s in LO_PEELED[B]) == (s in LO_ON_DVE) for s in range(LO_AHEAD))

    def lo_on_dve(k, s):
        return s in LO_PEELED.get(k, LO_ON_DVE)

    def lows(c, s, dve):
        return (before(c, lambda k: sum(lo_on_dve(k, t) == dve for t in active(k)))
                + sum(lo_on_dve(c.k, t) == dve for t in active(c.k) if t < s))

    def wait_low(eng, c, s):
        dve = lo_on_dve(c.k, s)
        eng.wait_ge(lo_sem[dve], lows(c, s, dve) + 1)

    def phases_before(c, f):
        return (before(c, lambda k: len(active(k)) // NT)
                + sum(c.has(LAG[g]) for g in PHASE_AT if PHASE_AT[g] < PHASE_AT[f]))

    JOBS = [("E", 0), ("D", 2), ("A", 1)]
    SPLITS = [("B", 1), ("E", 0), ("D", 2), ("A", 1)]
    NHTS = [("B", 1), ("D", 2), ("A", 1)]
    STAGES = [("B_nhT", 1), ("E_hT", 0), ("E_e", 0), ("D_H", 2), ("D_nhT", 2), ("A_H", 1),
              ("B_z", 0), ("A_nhT", 1), ("B_hT", 0), ("C_out", 2), ("B_H", 0)]

    STAGES_1 = ["B_nhT", "E_hT", "E_e", "A_H", "A_nhT", "B_z", "B_hT", "B_H"]

    def nth(events, c, name):
        n = before(c, lambda k: sum(0 <= k - lag < B for _, lag in events))
        if events is STAGES and c.k == 1:
            return n + STAGES_1.index(name)
        for e, lag in events:
            if e == name:
                return n
            n = n + int(c.has(lag))
        return n

    ctx = ExitStack()
    with ctx:
        def sb(name, shape, dt=F32):
            return ctx.enter_context(nc.sbuf_tensor(name, shape, dt))

        def sem(name):
            return ctx.enter_context(nc.semaphore(name))

        adj_sb = sb("adj_sb", [P, max(ADJ_SLOT) + 1, N])
        adjt_sb = [sb(f"adjt_sb{p}", [P, NT, N]) for p in range(2)]
        ew = sb("ew", [P, 2, N])
        mov_hi = sb("mov_hi", [P, RING, N], F32R)
        mov_lo = sb("mov_lo", [P, RING, N], F32R)
        sta_hi = [sb(f"sta_hi{i}", [P, N], F32R) for i in range(2)]
        sta_lo = [sb(f"sta_lo{i}", [P, N], F32R) for i in range(2)]
        nht_hi = [sb(f"nht_hi{i}", [P, N], F32R) for i in range(2)]
        nht_lo = [sb(f"nht_lo{i}", [P, N], F32R) for i in range(2)]
        x_sb = sb("x_sb", [P, NT, D])
        x1_sb = sb("x1_sb", [P, NT, D])
        park = [sb(f"park{p}", [P, NT, D]) for p in range(2)]
        yt = sb("yt", [P, N])
        val = [sb(f"val{i}", [P, NT, D]) for i in range(2)]
        scr = [sb(f"scr{i}", [P, NT, D]) for i in range(2)]
        e_sb = sb("e_sb", [P, NT, D])
        cst = sb("cst", [P, consts.shape[1]])
        deg = sb("deg", [P, NT])
        rdeg = sb("rdeg", [P, NT])
        rsum, ssum, var, root, inv, est, rstd = (
            [sb(f"{name}{i}", [P, NT]) for i in range(2)]
            for name in ("rsum", "ssum", "var", "root", "inv", "est", "rstd"))

        w = [cst[:, i * D:(i + 1) * D] for i in range(3)]
        wa_t, wb_t = cst[:, 3 * D:4 * D], cst[:, 4 * D:5 * D]
        bias = [cst[:, (5 + i) * D:(6 + i) * D].unsqueeze(1).to_broadcast([P, HT, D]) for i in range(3)]
        bias_l0 = cst[:, 8 * D:9 * D].unsqueeze(1).to_broadcast([P, HT, D])
        ident = cst[:, 9 * D:10 * D]

        gram = ctx.enter_context(nc.psum_tensor("gram", [P, 2, N], F32))
        ysum = ctx.enter_context(nc.psum_tensor("ysum", [P, N], F32))
        stage = ctx.enter_context(nc.psum_tensor("stage", [P, NT, D], F32))

        def by_half(name):
            return [sem(f"{name}_h{h}") for h in range(2)]

        def by_set(name):
            return [by_half(f"{name}{i}") for i in range(2)]

        const_in = sem("const_in")
        x_in = by_half("x_in")
        adj_in = [sem(f"adj_in{g}") for g in range(PAIRS)]
        adjt_in = [[sem(f"adjt_in{p}_{g}") for g in range(PAIRS)] for p in range(2)]
        parked = sem("parked")
        out_done = sem("out_done")
        cos_done = sem("cos_done")
        ew_done = sem("ew_done")
        hi_done = sem("hi_done")
        lo_dve = sem("lo_dve")
        lo_pool = sem("lo_pool")
        lo_sem = {True: lo_dve, False: lo_pool}
        hi_summed = sem("hi_summed")
        item_done = sem("item_done")
        y_read = by_half("y_read")
        stage_full = by_half("stage_full")
        stage_read = by_half("stage_read")
        rsum_done = by_half("rsum_done")
        centred = by_set("centred")
        sq_done = by_set("sq_done")
        ss_done = by_set("ss_done")
        nrm_done = by_set("nrm_done")
        var_done = [sem(f"var_done{i}") for i in range(2)]
        root_done = [sem(f"root_done{i}") for i in range(2)]
        newton = [sem(f"newton{i}") for i in range(2)]
        sta_hi_done = by_half("sta_hi_done")
        sta_lo_done = by_half("sta_lo_done")
        nht_hi_done = by_half("nht_hi_done")
        h_done = by_half("h_done")
        rdeg_done = sem("rdeg_done")
        x1_done = by_half("x1_done")

        def tiles(ap):
            return ap.rearrange("p (t d) -> p t d", d=D)

        def rows(dram, b):
            return dram[b].rearrange("(t p) d -> p t d", p=P)

        def run(eng, cycle):
            for k in (0, 1):
                cycle(Cycle(k))
            with eng.Fori(0, (B - 2) // 2) as i:
                for k in (2, 3):
                    cycle(Cycle(k, i))
            for k in range(B, LAST + 1):
                cycle(Cycle(k))

        def at(c, s):
            c, s = (c, s) if s < SLOTS else (c.next(), s - SLOTS)
            return (c, s) if s in active(c.k) else None

        def steps_of(slots, peeled):
            def due(name, c, s):
                return s == peeled.get(c.k, {}).get(name, slots[name])
            return due

        block = ctx.enter_context(nc.Block())

        @block.sync
        def _(sp):
            def cycle(c):
                if c.has(0):
                    b = c.graph(0)
                    if c.k > 0:
                        sp.wait_ge(x1_done[1], b)
                    for h, ts, _ in HALVES:
                        sp.dma_start(x_sb[:, ts, :], rows(x, b)[:, ts, :]).then_inc(x_in[h], 16)
                    if c.k > 0:
                        sp.wait_ge(item_done, item_end(c))
                    for g in range(PAIRS):
                        first = ADJ_SLOT[2 * g]
                        if first in ADJ_SLOT[:2 * g]:
                            at_slot = PHASE_AT[0] + ADJ_SLOT.index(first) + 1
                            sp.wait_ge(lo_dve, lows(c, at_slot, True) + 1)
                        sp.dma_start(adj_sb[:, first:first + 2, :],
                                     rows(adj, b)[:, 2 * g:2 * g + 2, :]).then_inc(adj_in[g], 16)
                        if c.k == 0 and g == 0:
                            sp.dma_start(cst[:, :], consts[:, :]).then_inc(const_in, 16)
                    for g in range(PAIRS):
                        if c.has(2):
                            sp.wait_ge(ew_done, cos_item(c, PHASE_AT[3] + 2 * g + 1) + 1)
                        sp.dma_start(adjt_sb[c.k % 2][:, 2 * g:2 * g + 2, :],
                                     rows(adj_t, b)[:, 2 * g:2 * g + 2, :])\
                            .then_inc(adjt_in[c.k % 2][g], 16)
                if c.has(2):
                    sp.wait_ge(stage_read[1], nth(STAGES, c, "C_out") + 1)
                    sp.dma_start(rows(out, c.graph(2)), park[c.k % 2][:, :, :]).then_inc(out_done, 16)
                if c.has(0):
                    if c.has(2):
                        sp.wait_ge(out_done, 16 * (c.graph(2) + 1))
                    else:
                        sp.wait_ge(x1_done[1], c.graph(0) + 1)
                    sp.dma_start(park[c.k % 2][:, :, :], x1_sb[:, :, :]).then_inc(parked, 16)

            def item_end(c):
                return before(c, lambda k: len(active(k)))

            run(sp, cycle)
            sp.wait_ge(out_done, 16 * B)

        @block.tensor
        def _(pe):
            due = steps_of(PE_AT, PE_PEELED)

            def cosines(now, c, s):
                q, f = s % NT, phase_of(s)
                hi, lo = nht_hi[f % 2], nht_lo[f % 2]
                n = cos_item(c, s)
                if not (c.i is None and n < 2):
                    pe.wait_ge(ew_done, n - 1)
                cols = slice(q * P, (q + 1) * P)
                parts = [slice(h * HALF, (h + 1) * HALF) for h in range(2)]
                products = [(lo, hi), (hi, lo), (hi, hi)]
                if q == 0:
                    order = [(p, h) for h in range(2) for p in products]
                else:
                    order = [(p, h) for p in products for h in range(2)]
                for (sta, mov), h in order:
                    if q == 0 and (sta, mov) == products[0]:
                        made = {2: "A_nhT", 1: "B_nhT", 3: "D_nhT"}[f]
                        pe.wait_ge(stage_read[h], nth(STAGES, now if f == 2 else c, made) + 1)
                    mm = nc.tensor.matmul(gram[:, q % 2, parts[h]], sta[:, cols], mov[:, parts[h]],
                                          start=(sta is lo), stop=(sta is hi and mov is hi))
                mm.then_inc(cos_done, 1)

            def sum_high(c, s):
                q, f = s % NT, phase_of(s)
                if q % HT == 0:
                    n = {2: nth(SPLITS, c, "B"), 1: nth(SPLITS, c, "B") + 1,
                         0: nth(SPLITS, c, "E") + 1, 3: nth(SPLITS, c, "D") + 1}[f]
                    pe.wait_ge(sta_hi_done[q // HT], n)
                    pe.wait_ge(sta_lo_done[q // HT], n)
                pe.wait_ge(hi_done, item(c, s) + 1)
                hi, lo = sta_hi[f % 2], sta_lo[f % 2]
                if q == 0:
                    order = [(hi, 0), (lo, 0), (hi, 1), (lo, 1)]
                else:
                    order = [(hi, 0), (hi, 1), (lo, 0), (lo, 1)]
                for sta, h in order:
                    if q == 0 and sta is hi and not (c.i is None and phases_before(c, f) == 0):
                        pe.wait_ge(y_read[h], phases_before(c, f))
                    part = slice(h * HALF, (h + 1) * HALF)
                    mm = nc.tensor.matmul(ysum[:, part], sta[:, q * P:(q + 1) * P],
                                          mov_hi[:, q % RING, part],
                                          start=(q == 0 and sta is hi), stop=False)
                mm.then_inc(hi_summed, 1)

            def sum_low(c, s):
                q, f = s % NT, phase_of(s)
                wait_low(pe, c, s)
                for h in range(2):
                    part = slice(h * HALF, (h + 1) * HALF)
                    mm = nc.tensor.matmul(ysum[:, part], sta_hi[f % 2][:, q * P:(q + 1) * P],
                                          mov_lo[:, q % RING, part], start=False, stop=(q == NT - 1))
                mm.then_inc(item_done, 1)

            def product(c, name, operand, wait):
                n = nth(STAGES, c, name)
                for h, ts, _ in HALVES:
                    if not (c.i is None and n == 0):
                        pe.wait_ge(stage_read[h], n)
                    if wait is not None:
                        pe.wait_ge(wait[0][h], wait[1])
                    for t in range(NT)[ts]:
                        src = operand(t, slice(t * P, (t + 1) * P))
                        if isinstance(src, tuple):
                            mm = nc.tensor.matmul(stage[:, t, :], src[0], src[1], start=True, stop=True)
                        else:
                            mm = nc.tensor.transpose(stage[:, t, :], src, ident)
                    mm.then_inc(stage_full[h], 1)

            def cycle(c):
                for s in range(SLOTS):
                    if at(c, s):
                        sum_high(c, s)
                        if s % NT > 0:
                            sum_low(c, s - 1)
                        if s % NT == NT - 1:
                            sum_low(c, s)
                    if (ahead := at(c, s + COS_AHEAD)) and is_cos(ahead[1]):
                        cosines(c, *ahead)
                    if due("B_nhT", c, s) and c.has(1):
                        product(c, "B_nhT", lambda t, cols: scr[1][:, t, :],
                                (nrm_done[1], 2 * c.graph(1) + 2))
                    if due("E_hT", c, s) and c.has(0):
                        if c.k == 0:
                            pe.wait_ge(const_in, 16)
                        product(c, "E_hT", lambda t, cols: val[0][:, t, :], (h_done, c.graph(0) + 1))
                    if due("E_e", c, s) and c.has(0):
                        product(c, "E_e", lambda t, cols: (e_sb[:, t, :], wa_t), None)
                    if due("D_H", c, s) and c.has(2):
                        product(c, "D_H", lambda t, cols: (yt[:, cols], w[2]),
                                (y_read, phases_before(c, 1)))
                    if due("D_nhT", c, s) and c.has(2):
                        product(c, "D_nhT", lambda t, cols: scr[0][:, t, :],
                                (nrm_done[0], nth(JOBS, c, "D") + 1))
                    if due("A_H", c, s) and c.has(1):
                        product(c, "A_H", lambda t, cols: (yt[:, cols], w[1]),
                                (y_read, phases_before(c, 0)))
                    if due("B_z", c, s) and c.has(0):
                        product(c, "B_z", lambda t, cols: (yt[:, cols], wb_t),
                                (y_read, phases_before(c, 3)))
                    if due("A_nhT", c, s) and c.has(1):
                        product(c, "A_nhT", lambda t, cols: scr[0][:, t, :],
                                (nrm_done[0], nth(JOBS, c, "A") + 1))
                    if due("B_hT", c, s) and c.has(0):
                        product(c, "B_hT", lambda t, cols: scr[1][:, t, :],
                                (nrm_done[1], 2 * c.graph(0) + 1))
                    if due("C_out", c, s) and c.has(2):
                        product(c, "C_out", lambda t, cols: yt[:, cols],
                                (y_read, phases_before(c, 3) + 1))
                    if due("B_H", c, s) and c.has(0):
                        product(c, "B_H", lambda t, cols: (e_sb[:, t, :], w[0]), None)

            run(pe, cycle)

        @block.vector
        def _(dve):
            due = steps_of(DVE_AT, DVE_PEELED)

            def times_adj(c, s):
                q, f = s % NT, phase_of(s)
                parity = (c.k - LAG[f]) % 2
                if f == 1 and q % 2 == 0:
                    dve.wait_ge(adjt_in[parity][q // 2],
                                16 * ((c.k - 1) // 2 + 1 + (0 if c.i is None else c.i)))
                dve.wait_ge(cos_done, cos_item(c, s) + 1)
                before_s = [t for t in active(c.k) if is_cos(t) and t < s]
                if len(before_s) >= 2:
                    wait_low(dve, c, before_s[-2])
                elif not (c.i is None and cos_item(c, s) < 2):
                    for on_dve, done in ((False, lo_pool), (True, lo_dve)):
                        prior = c.k - 1 if c.i is None else 3
                        of_last = 0 if before_s else int(lo_on_dve(prior, SLOTS - 1) == on_dve)
                        dve.wait_ge(done, lows(c, 0, on_dve) - of_last)
                nc.vector.tensor_tensor(ew[:, q % 2, :], adjt_sb[parity][:, q, :], gram[:, q % 2, :],
                                        ALU.mult).then_inc(ew_done, 1)

            def low_part(c, s):
                q = s % NT
                n = item(c, s)
                dve.wait_ge(hi_done, n + 1)
                if not (c.i is None and n < RING):
                    dve.wait_ge(item_done, n - RING + 1)
                src = ew[:, q % 2, :] if is_cos(s) else adj_sb[:, ADJ_SLOT[q], :]
                nc.vector.tensor_tensor(mov_lo[:, q % RING, :], src, mov_hi[:, q % RING, :].bitcast(F32),
                                        ALU.subtract).then_inc(lo_dve, 1)

            def bc(stat, ts):
                return stat[:, ts].unsqueeze(2).to_broadcast([P, HT, D])

            def val_free(c, splits):
                if not (c.i is None and splits == 0):
                    dve.wait_ge(sta_hi_done[1], splits)
                    dve.wait_ge(sta_lo_done[1], splits)

            def centre(i, n, src, summed):
                for h, ts, _ in HALVES:
                    dve.wait_ge(summed[h], n)
                    nc.vector.scalar_tensor_tensor(out=val[i][:, ts, :], in0=bc(rsum[i], ts),
                                                   scalar=-1.0 / D, in1=src[:, ts, :], op0=ALU.mult,
                                                   op1=ALU.add)\
                        .then_inc(centred[i][h], 1)

            def variance(i, n, layernorm):
                for h, ts, _ in HALVES:
                    dve.wait_ge(sq_done[i][h], n)
                    nc.vector.tensor_reduce(ssum[i][:, ts], scr[i][:, ts, :], AX, ALU.add)\
                        .then_inc(ss_done[i][h], 1)
                dve.wait_ge(ss_done[i][1], n)
                if layernorm:
                    nc.vector.tensor_scalar(var[i][:, :], ssum[i][:, :], 1.0 / D, LN_EPS, ALU.mult,
                                            ALU.add).then_inc(var_done[i], 1)
                else:
                    nc.vector.tensor_scalar(var[i][:, :], ssum[i][:, :], NORM_EPS * NORM_EPS, None,
                                            ALU.max).then_inc(var_done[i], 1)

            def normalise(i, n):
                dve.wait_ge(root_done[i], n)
                nc.vector.reciprocal(inv[i][:, :], root[i][:, :]).then_inc(newton[i], 1)
                dve.wait_ge(newton[i], 4 * n - 3)
                nc.vector.tensor_tensor(est[i][:, :], inv[i][:, :], var[i][:, :], ALU.mult)\
                    .then_inc(newton[i], 1)
                dve.wait_ge(newton[i], 4 * n - 2)
                nc.vector.tensor_tensor(inv[i][:, :], est[i][:, :], root[i][:, :], ALU.add)\
                    .then_inc(newton[i], 1)
                dve.wait_ge(newton[i], 4 * n - 1)
                nc.vector.reciprocal(rstd[i][:, :], inv[i][:, :]).then_inc(newton[i], 1)
                dve.wait_ge(newton[i], 4 * n)
                for h, ts, _ in HALVES:
                    nc.vector.scalar_tensor_tensor(out=scr[i][:, ts, :], in0=val[i][:, ts, :], scalar=2.0,
                                                   in1=bc(rstd[i], ts), op0=ALU.mult, op1=ALU.mult)\
                        .then_inc(nrm_done[i][h], 1)

            def add_bias(n, dst, b):
                for h, ts, _ in HALVES:
                    dve.wait_ge(stage_full[h], n + 1)
                    nc.vector.tensor_tensor(dst[:, ts, :], stage[:, ts, :], b, ALU.add)\
                        .then_inc(stage_read[h], 1)

            def make_h(c, stage_name, i, b):
                add_bias(nth(STAGES, c, stage_name), val[i], b)

            def nht_low(c, stage_name, name, i):
                for h, ts, cols in HALVES:
                    dve.wait_ge(nht_hi_done[h], nth(NHTS, c, name) + 1)
                    nc.vector.tensor_tensor(tiles(nht_lo[i][:, cols]), stage[:, ts, :],
                                            tiles(nht_hi[i][:, cols]).bitcast(F32), ALU.subtract)\
                        .then_inc(stage_read[h], 1)

            def cycle(c):
                for s in range(SLOTS):
                    if (ahead := at(c, s + HI_AHEAD)) and is_cos(ahead[1]):
                        times_adj(*ahead)
                    if (ahead := at(c, s + LO_AHEAD)) and lo_on_dve(ahead[0].k, ahead[1]):
                        low_part(*ahead)
                    if due("B_make", c, s) and c.has(1):
                        add_bias(prior_stages(c) - 1, val[1], bias[0])
                    if due("B_var", c, s) and c.has(1):
                        variance(1, 2 * c.graph(1) + 2, False)
                    if due("B_nrm", c, s) and c.has(1):
                        normalise(1, 2 * c.graph(1) + 2)
                    if due("B_low", c, s) and c.has(1):
                        nht_low(c, "B_nhT", "B", 1)
                    if due("E_sum", c, s) and c.has(0):
                        for h, ts, _ in HALVES:
                            dve.wait_ge(x_in[h], 16 * (c.graph(0) + 1))
                            nc.vector.tensor_reduce(rsum[0][:, ts], x_sb[:, ts, :], AX, ALU.add)\
                                .then_inc(rsum_done[h], 1)
                    if due("E_val", c, s) and c.has(0):
                        val_free(c, nth(SPLITS, c, "E"))
                        centre(0, c.graph(0) + 1, x_sb, rsum_done)
                    if due("E_var", c, s) and c.has(0):
                        variance(0, nth(JOBS, c, "E") + 1, True)
                    if due("E_nrm", c, s) and c.has(0):
                        normalise(0, nth(JOBS, c, "E") + 1)
                    if due("E_nrm", c, s) and c.k == 0:
                        for h, ts, cols in HALVES:
                            dve.wait_ge(sta_hi_done[h], 1)
                            nc.vector.tensor_tensor(tiles(sta_lo[0][:, cols]), val[0][:, ts, :],
                                                    tiles(sta_hi[0][:, cols]).bitcast(F32), ALU.subtract)\
                                .then_inc(sta_lo_done[h], 1)
                    if due("E_e", c, s) and c.has(0):
                        if c.k == 0:
                            dve.wait_ge(const_in, 16)
                        add_bias(nth(STAGES, c, "E_e"), e_sb, bias_l0)
                    if due("D_make", c, s) and c.has(2):
                        val_free(c, nth(SPLITS, c, "D"))
                        make_h(c, "D_H", 0, bias[2])
                    if due("D_var", c, s) and c.has(2):
                        variance(0, nth(JOBS, c, "D") + 1, False)
                    if due("D_nrm", c, s) and c.has(2):
                        normalise(0, nth(JOBS, c, "D") + 1)
                    if due("D_low", c, s) and c.has(2):
                        nht_low(c, "D_nhT", "D", 1)
                    if due("A_make", c, s) and c.has(1):
                        val_free(c, nth(SPLITS, c, "A"))
                        make_h(c, "A_H", 0, bias[1])
                    if due("A_var", c, s) and c.has(1):
                        variance(0, nth(JOBS, c, "A") + 1, False)
                    if due("A_nrm", c, s) and c.has(1):
                        normalise(0, nth(JOBS, c, "A") + 1)
                    if due("A_low", c, s) and c.has(1):
                        nht_low(c, "A_nhT", "A", 0)
                    if due("B_z", c, s) and c.has(0):
                        b = c.graph(0)
                        dve.wait_ge(y_read[0], phases_before(c, 3))
                        nc.vector.reciprocal(rdeg[:, :], deg[:, :]).then_inc(rdeg_done, 1)
                        dve.wait_ge(rdeg_done, b + 1)
                        for h, ts, _ in HALVES:
                            dve.wait_ge(stage_full[h], nth(STAGES, c, "B_z") + 1)
                            for t in range(NT)[ts]:
                                z = nc.vector.scalar_tensor_tensor(
                                    out=scr[1][:, t, :], in0=stage[:, t, :], scalar=rdeg[:, t:t + 1],
                                    in1=e_sb[:, t, :], op0=ALU.mult, op1=ALU.add)
                            z.then_inc(stage_read[h], 1)
                    if due("B_x1", c, s) and c.has(0):
                        b = c.graph(0)
                        if c.k > 0:
                            dve.wait_ge(parked, 16 * b)
                        for h, ts, _ in HALVES:
                            dve.wait_ge(stage_read[h], nth(STAGES, c, "B_z") + 1)
                            for t in range(NT)[ts]:
                                x1 = nc.vector.scalar_tensor_tensor(
                                    out=x1_sb[:, t, :], in0=scr[1][:, t, :], scalar=0.0, in1=x_sb[:, t, :],
                                    op0=ALU.max, op1=ALU.add, accum_out=rsum[1][:, t:t + 1])
                            x1.then_inc(x1_done[h], 1)
                    if due("B_val", c, s) and c.has(0):
                        if c.has(1):
                            val_free(c, nth(SPLITS, c, "B") + 1)
                        centre(1, c.graph(0) + 1, x1_sb, x1_done)
                    if due("B_var1", c, s) and c.has(0):
                        variance(1, 2 * c.graph(0) + 1, True)
                    if due("B_nrm1", c, s) and c.has(0):
                        normalise(1, 2 * c.graph(0) + 1)
                    if due("C_out", c, s) and c.has(2):
                        b = c.graph(2)
                        dve.wait_ge(parked, 16 * (b + 1))
                        for h, ts, _ in HALVES:
                            dve.wait_ge(stage_full[h], nth(STAGES, c, "C_out") + 1)
                            nc.vector.tensor_tensor(park[c.k % 2][:, ts, :], stage[:, ts, :],
                                                    park[c.k % 2][:, ts, :], ALU.add)\
                                .then_inc(stage_read[h], 1)

            def prior_stages(c):
                return before(c, lambda k: sum(0 <= k - lag < B for _, lag in STAGES))

            run(dve, cycle)

        @block.scalar
        def _(act):
            due = steps_of(ACT_AT, ACT_PEELED)

            def high_part(c, s):
                q, n = s % NT, item(c, s)
                if is_cos(s):
                    act.wait_ge(ew_done, cos_item(c, s) + 1)
                    src = ew[:, q % 2, :]
                else:
                    if q % 2 == 0:
                        act.wait_ge(adj_in[q // 2], 16 * (c.graph(0) + 1))
                    src = adj_sb[:, ADJ_SLOT[q], :]
                if not (c.i is None and n < RING):
                    act.wait_ge(hi_summed, n - RING + 1)
                    pos = active(c.k).index(s)
                    old = active(c.k)[pos - RING] if pos >= RING else None
                    if c.k == 1 and pos < RING:
                        wait_low(act, Cycle(0), active(0)[pos - RING])
                    elif old is not None and not (is_cos(s) and is_cos(old)):
                        wait_low(act, c, old)
                if is_cos(s):
                    nc.scalar.activation(mov_hi[:, q % RING, :], src, ACT.Copy).then_inc(hi_done, 1)
                else:
                    nc.scalar.activation(mov_hi[:, q % RING, :], src, ACT.Identity,
                                         accum_out=deg[:, q:q + 1]).then_inc(hi_done, 1)

            def read_sum(c, f):
                s = PHASE_AT[f] + NT - 1
                act.wait_ge(item_done, item(c, s) + 1)
                prior = {2: "E_hT", 1: "A_H", 0: "A_nhT" if c.k == 1 else "B_z", 3: "C_out"}[f]
                n = nth(STAGES, c, prior)
                if not (c.i is None and n == 0):
                    act.wait_ge(stage_full[1], n)
                for h, _, cols in HALVES:
                    nc.scalar.activation(yt[:, cols], ysum[:, cols], ACT.Relu if f in (1, 2) else ACT.Copy)\
                        .then_inc(y_read[h], 1)

            def squares(i, made, n, read):
                for h, ts, _ in HALVES:
                    act.wait_ge(made[h], n)
                    if read is not None:
                        act.wait_ge(stage_full[h], read)
                    nc.scalar.activation(scr[i][:, ts, :], val[i][:, ts, :], ACT.Square)\
                        .then_inc(sq_done[i][h], 1)

            def square_root(i, n):
                act.wait_ge(var_done[i], n)
                nc.scalar.activation(root[i][:, :], var[i][:, :], ACT.Sqrt).then_inc(root_done[i], 1)

            def sta_high(i, v, n):
                if n is not None:
                    act.wait_ge(item_done, n)
                for h, ts, cols in HALVES:
                    nc.scalar.activation(tiles(sta_hi[i][:, cols]), val[v][:, ts, :], ACT.Copy)\
                        .then_inc(sta_hi_done[h], 1)

            def nht_high(c, stage_name, i):
                for h, ts, cols in HALVES:
                    act.wait_ge(stage_full[h], nth(STAGES, c, stage_name) + 1)
                    nc.scalar.activation(tiles(nht_hi[i][:, cols]), stage[:, ts, :], ACT.Copy)\
                        .then_inc(nht_hi_done[h], 1)

            def take_ht(c, stage_name, fn):
                for h, ts, _ in HALVES:
                    act.wait_ge(stage_full[h], nth(STAGES, c, stage_name) + 1)
                    nc.scalar.activation(e_sb[:, ts, :], stage[:, ts, :], fn).then_inc(stage_read[h], 1)

            def cycle(c):
                for s in range(SLOTS):
                    if ahead := at(c, s + HI_AHEAD):
                        high_part(*ahead)
                    if s == NT - 1 and c.has(2):
                        read_sum(c, 2)
                    if s == 2 * NT - 1 and c.has(1):
                        read_sum(c, 1)
                    if s == 3 * NT - 1 and c.has(0):
                        read_sum(c, 0)
                    if s == 4 * NT - 1 and c.has(2):
                        read_sum(c, 3)
                    if due("B_sq", c, s) and c.has(1):
                        n = before(c, lambda k: sum(0 <= k - lag < B for _, lag in STAGES))
                        squares(1, stage_read, n, None)
                    if due("B_root", c, s) and c.has(1):
                        square_root(1, 2 * c.graph(1) + 2)
                    if due("B_sta", c, s) and c.has(1):
                        sta_high(1, 1, items_before(c))
                    if due("B_high", c, s) and c.has(1):
                        nht_high(c, "B_nhT", 1)
                    if due("E_sq", c, s) and c.has(0):
                        squares(0, centred[0], c.graph(0) + 1, nth(STAGES, c, "E_hT") if c.k > 0 else None)
                    if due("E_root", c, s) and c.has(0):
                        square_root(0, nth(JOBS, c, "E") + 1)
                    if due("E_h", c, s) and c.has(0):
                        n = item(c, 7) + 1 if c.has(2) else items_before(c)
                        for h, ts, cols in HALVES:
                            act.wait_ge(nrm_done[0][h], nth(JOBS, c, "E") + 1)
                            nc.scalar.activation(val[0][:, ts, :], scr[0][:, ts, :], ACT.Relu)\
                                .then_inc(h_done[h], 1)
                            if c.k > 0 and h == 0:
                                act.wait_ge(item_done, n)
                            nc.scalar.activation(tiles(sta_hi[0][:, cols]), scr[0][:, ts, :], ACT.Relu)\
                                .then_inc(sta_hi_done[h], 1)
                    if due("E_hT", c, s) and c.has(0):
                        take_ht(c, "E_hT", ACT.Copy)
                    if due("D_sq", c, s) and c.has(2):
                        squares(0, stage_read, nth(STAGES, c, "D_H") + 1, None)
                    if due("D_root", c, s) and c.has(2):
                        square_root(0, nth(JOBS, c, "D") + 1)
                    if due("D_sta", c, s) and c.has(2):
                        sta_high(1, 0, item(c, 15) + 1 if c.has(1) else item(c, 7) + 1)
                    if due("D_high", c, s) and c.has(2):
                        nht_high(c, "D_nhT", 1)
                    if due("A_sq", c, s) and c.has(1):
                        squares(0, stage_read, nth(STAGES, c, "A_H") + 1, None)
                    if due("A_root", c, s) and c.has(1):
                        square_root(0, nth(JOBS, c, "A") + 1)
                    if due("A_sta", c, s) and c.has(1):
                        sta_high(0, 0, item(c, 23) + 1 if c.has(0) else item(c, 15) + 1)
                    if due("A_high", c, s) and c.has(1):
                        nht_high(c, "A_nhT", 0)
                    if due("B_sq1", c, s) and c.has(0):
                        squares(1, centred[1], c.graph(0) + 1, None)
                    if due("B_root1", c, s) and c.has(0):
                        square_root(1, 2 * c.graph(0) + 1)
                    if due("B_hT", c, s) and c.has(0):
                        take_ht(c, "B_hT", ACT.Relu)

            def items_before(c):
                return before(c, lambda k: len(active(k)))

            run(act, cycle)

        @block.gpsimd
        def _(pool):
            due = steps_of(POOL_AT, POOL_PEELED)

            def low_part(c, s):
                q, n = s % NT, item(c, s)
                pool.wait_ge(hi_done, n + 1)
                if not (c.i is None and n < RING):
                    pool.wait_ge(item_done, n - RING + 1)
                src = ew[:, q % 2, :] if is_cos(s) else adj_sb[:, ADJ_SLOT[q], :]
                nc.gpsimd.tensor_tensor(mov_lo[:, q % RING, :], src, mov_hi[:, q % RING, :].bitcast(F32),
                                        ALU.subtract).then_inc(lo_pool, 1)

            def sta_low(c, i, name):
                v = 1 if name == "B" else 0
                for h, ts, cols in HALVES:
                    pool.wait_ge(sta_hi_done[h], nth(SPLITS, c, name) + 1)
                    nc.gpsimd.tensor_tensor(tiles(sta_lo[i][:, cols]), val[v][:, ts, :],
                                            tiles(sta_hi[i][:, cols]).bitcast(F32), ALU.subtract)\
                        .then_inc(sta_lo_done[h], 1)

            def cycle(c):
                for s in range(SLOTS):
                    if (ahead := at(c, s + LO_AHEAD)) and not lo_on_dve(ahead[0].k, ahead[1]):
                        low_part(*ahead)
                    if due("B", c, s) and c.has(1):
                        sta_low(c, 1, "B")
                    if due("E", c, s) and 0 < c.k and c.has(0):
                        sta_low(c, 0, "E")
                    if due("D", c, s) and c.has(2):
                        sta_low(c, 1, "D")
                    if due("A", c, s) and c.has(1):
                        sta_low(c, 0, "A")

            run(pool, cycle)


def kernel(x, adj, L0_gnn_W, L0_gnn_b, L1_gnn_W0, L1_gnn_b0, L1_gnn_W1, L1_gnn_b1, L1_gnn_W2, L1_gnn_b2):
    import numpy as np
    import concourse.bacc as bacc
    from concourse.bass_utils import run_bass_kernel_spmd

    nc = bacc.Bacc("TRN2", target_bir_lowering=False, num_devices=1)
    x, adj, W = np.asarray(x), np.asarray(adj), np.asarray(L0_gnn_W)
    D = x.shape[2]
    consts = np.concatenate(
        [np.asarray(L1_gnn_W0), np.asarray(L1_gnn_W1), np.asarray(L1_gnn_W2), W[:, :D].T, W[:, D:].T]
        + [np.repeat(np.asarray(b)[None, :], P, axis=0)
           for b in (L1_gnn_b0, L1_gnn_b1, L1_gnn_b2, L0_gnn_b)]
        + [np.eye(P, dtype=np.float32)], axis=1)
    arrays = {
        "in_x": np.ascontiguousarray(x),
        "in_adj": np.ascontiguousarray(adj),
        "in_adj_t": np.ascontiguousarray(adj.transpose(0, 2, 1)),
        "in_consts": np.ascontiguousarray(consts),
    }
    args = [nc.dram_tensor(n, a.shape, mybir.dt.from_np(a.dtype), kind="ExternalInput").ap()
            for n, a in arrays.items()]
    out = nc.dram_tensor("out", x.shape, F32, kind="ExternalOutput").ap()
    build(nc, *args, out)
    r = run_bass_kernel_spmd(nc, [arrays], core_ids=[0])
    return r.results[0]["out"]
```
